# Optimizing a Trainium2 kernel written in Bass

```python
import numpy as np
import jax
import jax.numpy as jnp

def _softmax(x, axis=-1):
    return jax.nn.softmax(x, axis=axis)

def _gelu(x):
    return jax.nn.gelu(x, approximate=True)

def _silu(x):
    return jax.nn.silu(x)

def _sigmoid(x):
    return jax.nn.sigmoid(x)

def _layernorm(x, axis=-1, eps=1e-05):
    m = jnp.mean(x, axis=axis, keepdims=True)
    v = jnp.var(x, axis=axis, keepdims=True)
    return (x - m) / jnp.sqrt(v + eps)

def _scatter_add(tgt, idx, src, axis=0):
    return tgt.at[idx].add(src)

def _segment_sum(src, seg, n):
    return jax.ops.segment_sum(src, seg, n)
kernel_name = 'mk_recurrent_d1_jaxref_r8_af17d4'

def setup_inputs(seed: int=0):
    np.random.seed(seed)
    _w = jnp.asarray

    def _L0_attn_setup():
        import jax, jax.numpy as jnp
        import numpy as np
        B, S, H, NH, P = (1, 256, 128, 16, 2)
        D = H // NH
        SCALE = 1.0 / np.sqrt(D).astype(np.float32)

        def _lin(x, W, b):
            return x @ W + b

        def _split_heads(x):
            return x.reshape(*x.shape[:-2], x.shape[-2], NH, D).swapaxes(-3, -2)

        def _merge_heads(x):
            return x.swapaxes(-3, -2).reshape(*x.shape[:-3], x.shape[-2], H)
        key = jax.random.key(seed)
        ks = jax.random.split(key, 20)
        w = lambda k, i, o: jax.random.normal(k, (i, o), jnp.float32) * 0.02
        inp = {'hidden_states': jax.random.normal(ks[0], (B, S, H), jnp.float32), 'past_states': jax.random.normal(ks[1], (P, B, S, H), jnp.float32), 'Wq': w(ks[2], H, H), 'bq': jnp.zeros((H,), jnp.float32), 'Wk': w(ks[3], H, H), 'bk': jnp.zeros((H,), jnp.float32), 'Wv': w(ks[4], H, H), 'bv': jnp.zeros((H,), jnp.float32), 'Wo': w(ks[5], H, H), 'bo': jnp.zeros((H,), jnp.float32), 'Wrq': w(ks[6], H, H), 'brq': jnp.zeros((H,), jnp.float32), 'Wrk': w(ks[7], H, H), 'brk': jnp.zeros((H,), jnp.float32), 'Wrv': w(ks[8], H, H), 'brv': jnp.zeros((H,), jnp.float32), 'Wg': w(ks[9], 2 * H, H), 'bg': jnp.zeros((H,), jnp.float32)}
        return inp
    _L0_attn_in = _L0_attn_setup()

    def _L0_ffn_setup():
        import jax, jax.numpy as jnp
        import numpy as np
        DIM = 128
        HIDDEN = 384
        SCALE = 1.0 / 127.0

        def _dequant(w_int, dtype):
            return w_int.astype(dtype) * jnp.asarray(SCALE, dtype)
        key = jax.random.key(seed)
        k_x, k_g, k_u, k_d = jax.random.split(key, 4)
        x = jax.random.normal(k_x, (4, 256, DIM), dtype=jnp.float32)
        w_gate = jax.random.randint(k_g, (HIDDEN, DIM), -127, 128, dtype=jnp.int32)
        w_up = jax.random.randint(k_u, (HIDDEN, DIM), -127, 128, dtype=jnp.int32)
        w_down = jax.random.randint(k_d, (DIM, HIDDEN), -127, 128, dtype=jnp.int32)
        return {'x': x, 'w_gate': w_gate, 'w_up': w_up, 'w_down': w_down}
    _L0_ffn_in = _L0_ffn_setup()
    _d = {'L0_attn_hidden_states': _L0_attn_in['hidden_states'], 'L0_attn_past_states': _L0_attn_in['past_states'], 'L0_attn_Wq': _L0_attn_in['Wq'], 'L0_attn_bq': _L0_attn_in['bq'], 'L0_attn_Wk': _L0_attn_in['Wk'], 'L0_attn_bk': _L0_attn_in['bk'], 'L0_attn_Wv': _L0_attn_in['Wv'], 'L0_attn_bv': _L0_attn_in['bv'], 'L0_attn_Wo': _L0_attn_in['Wo'], 'L0_attn_bo': _L0_attn_in['bo'], 'L0_attn_Wrq': _L0_attn_in['Wrq'], 'L0_attn_brq': _L0_attn_in['brq'], 'L0_attn_Wrk': _L0_attn_in['Wrk'], 'L0_attn_brk': _L0_attn_in['brk'], 'L0_attn_Wrv': _L0_attn_in['Wrv'], 'L0_attn_brv': _L0_attn_in['brv'], 'L0_attn_Wg': _L0_attn_in['Wg'], 'L0_attn_bg': _L0_attn_in['bg'], 'L0_ffn_w_gate': _L0_ffn_in['w_gate'], 'L0_ffn_w_up': _L0_ffn_in['w_up'], 'L0_ffn_w_down': _L0_ffn_in['w_down']}
    _x0 = _d['L0_attn_hidden_states']
    _d['L0_attn_hidden_states'] = jax.random.normal(jax.random.fold_in(jax.random.key(seed), 1), (16, 512, 128), dtype=_x0.dtype)
    del _x0
    return _d

def reference(L0_attn_hidden_states, L0_attn_past_states, L0_attn_Wq, L0_attn_bq, L0_attn_Wk, L0_attn_bk, L0_attn_Wv, L0_attn_bv, L0_attn_Wo, L0_attn_bo, L0_attn_Wrq, L0_attn_brq, L0_attn_Wrk, L0_attn_brk, L0_attn_Wrv, L0_attn_brv, L0_attn_Wg, L0_attn_bg, L0_ffn_w_gate, L0_ffn_w_up, L0_ffn_w_down):

    def _L0_attn_ref(hidden_states, past_states, Wq, bq, Wk, bk, Wv, bv, Wo, bo, Wrq, brq, Wrk, brk, Wrv, brv, Wg, bg):
        import jax, jax.numpy as jnp
        import numpy as np
        B, S, H, NH, P = (1, 256, 128, 16, 2)
        D = H // NH
        SCALE = 1.0 / np.sqrt(D).astype(np.float32)

        def _lin(x, W, b):
            return x @ W + b

        def _split_heads(x):
            return x.reshape(*x.shape[:-2], x.shape[-2], NH, D).swapaxes(-3, -2)

        def _merge_heads(x):
            return x.swapaxes(-3, -2).reshape(*x.shape[:-3], x.shape[-2], H)
        q = _split_heads(_lin(hidden_states, Wq, bq))
        k = _split_heads(_lin(hidden_states, Wk, bk))
        v = _split_heads(_lin(hidden_states, Wv, bv))
        scores = jnp.einsum('bhsd,bhtd->bhst', q, k) * SCALE
        attn = jax.nn.softmax(scores, axis=-1)
        ctx = jnp.einsum('bhst,bhtd->bhsd', attn, v)
        output = _lin(_merge_heads(ctx), Wo, bo)
        rq = _split_heads(_lin(output, Wrq, brq))
        rk = _split_heads(_lin(past_states, Wrk, brk))
        rv = _split_heads(_lin(past_states, Wrv, brv))
        rscores = jnp.einsum('bhsd,pbhtd->pbhst', rq, rk) * SCALE
        rattn = jax.nn.softmax(rscores, axis=-1)
        rctx = jnp.einsum('pbhst,pbhtd->pbhsd', rattn, rv)
        recursive_output = _merge_heads(rctx).mean(axis=0)
        gate = jax.nn.sigmoid(_lin(jnp.concatenate([output, recursive_output], axis=-1), Wg, bg))
        output = output * (1.0 - gate) + recursive_output * gate
        return output

    def _L0_ffn_ref(x, w_gate, w_up, w_down):
        import jax, jax.numpy as jnp
        import numpy as np
        DIM = 128
        HIDDEN = 384
        SCALE = 1.0 / 127.0

        def _dequant(w_int, dtype):
            return w_int.astype(dtype) * jnp.asarray(SCALE, dtype)
        wg = _dequant(w_gate, x.dtype)
        wu = _dequant(w_up, x.dtype)
        wd = _dequant(w_down, x.dtype)
        gate = jnp.einsum('bsd,hd->bsh', x, wg)
        up = jnp.einsum('bsd,hd->bsh', x, wu)
        h = jax.nn.silu(gate) * up
        return jnp.einsum('bsh,dh->bsd', h, wd)
    x = L0_attn_hidden_states
    xn = _layernorm(x, axis=-1)
    s = _L0_attn_ref(xn, L0_attn_past_states, L0_attn_Wq, L0_attn_bq, L0_attn_Wk, L0_attn_bk, L0_attn_Wv, L0_attn_bv, L0_attn_Wo, L0_attn_bo, L0_attn_Wrq, L0_attn_brq, L0_attn_Wrk, L0_attn_brk, L0_attn_Wrv, L0_attn_brv, L0_attn_Wg, L0_attn_bg)
    g = _silu(_L0_ffn_ref(xn, L0_ffn_w_gate, L0_ffn_w_up, L0_ffn_w_down))
    x = x + s * g
    return x

_drawn_inputs = setup_inputs


def setup_inputs(seed=0):
    import zlib

    import numpy as np

    out = dict(_drawn_inputs(seed))
    spreads = {'L0_attn_bq': (0.0, 0.8),
     'L0_attn_bk': (0.0, 0.8),
     'L0_attn_bv': (0.0, 0.1),
     'L0_attn_bo': (0.0, 0.1),
     'L0_attn_brq': (0.0, 0.8),
     'L0_attn_brk': (0.0, 0.8),
     'L0_attn_brv': (0.0, 0.1),
     'L0_attn_bg': (0.0, 0.1)}
    factors = {'L0_attn_Wq': 8.0,
     'L0_attn_Wk': 8.0,
     'L0_attn_Wv': 3.537,
     'L0_attn_Wrq': 8.0,
     'L0_attn_Wrk': 8.0,
     'L0_attn_Wg': 3.624}
    for name, (base, spread) in spreads.items():
        noise = np.random.default_rng([zlib.crc32(name.encode()), seed]).standard_normal(out[name].shape)
        drawn = base * np.exp(spread * noise) if base else spread * noise
        out[name] = jnp.asarray(drawn.astype(out[name].dtype))
    for name, factor in factors.items():
        out[name] = (out[name] * factor).astype(out[name].dtype)
    return out
```

```python
from contextlib import ExitStack

import concourse.bass as bass
from concourse import mybir

F32 = mybir.dt.float32
BF16 = mybir.dt.bfloat16
I32 = mybir.dt.int32
ALU = mybir.AluOpType
ACT = mybir.ActivationFunctionType
AX_X = mybir.AxisListType.X

BATCH = 16
S = 512
H = 128
HEADS = 16
D = H // HEADS
PAST = 2
HIDDEN = 384
NB = HIDDEN // 128
ST = S // 128
SCALE = 1.0 / float(D) ** 0.5
DEQUANT = 0.007874015718698502
EPS = 1e-5

PARTS = 3
ROWS = 6 * D
MAXROW = ROWS
QUAD = 4
GROUPS = HEADS // QUAD
FIRST_HEAD = [0, 8, 4, 12]
PAIRS = HEADS // 2
BEATS = GROUPS * ST
TILES = QUAD * BEATS
RING = 3
PBUF = 4
SLOT = D + 1



class Count:

    def __init__(self, a, c):
        self.a, self.c = a, c

    def __add__(self, n):
        return Count(self.a, self.c + n)

    def __sub__(self, n):
        return Count(self.a, self.c - n)

    def __mul__(self, n):
        return Count(self.a * n, self.c * n)

    __rmul__ = __mul__

    def __gt__(self, n):
        assert not (self.c <= n and self.a > 0), "zero in the first turn"
        return self.c > n

    def at(self, turn):
        return self.c if turn is None else turn * self.a + self.c


def stage(kind, i):
    if kind == "own":
        return Count(0, 0) if i.a == 0 and i.c == 0 else 2 * i - 1
    return Count(0, 31) if i.a == 0 and i.c == BATCH - 1 else 2 * i + 2


def in_ring(s, t):
    return TILES * s + (t - (RING - 1) if t >= RING else (0, -2, -1)[t])


PLAIN = {b: [b] for b in range(BEATS)}


class Slot:

    def __init__(self, probs, maxima, small, pool, sync, stats=None, plan=None):
        self.probs, self.maxima, self.small = probs, maxima, small
        self.pool, self.sync, self.stats = pool, sync, stats
        self.plan = plan or PLAIN


def odd_slot(i, first=False, last=False):
    small = {2: ("max own 1", i), 6: ("ffn y", i), 9: ("max past 0", i - 1), 10: ("ctx own 0", i)}
    pool = [("max own 1", i)]
    sync = [("max own 1", i)]
    if not last:
        small.update({3: ("xnT", i + 1), 4: ("q", i + 1), 5: ("k", i + 1), 8: ("v", i + 1)})
        pool += [("xn", i + 1)]
    if not first:
        small.update({1: ("ctx past 3", i - 2), 7: ("rctxT", i - 2), 11: ("gate", i - 2), 14: ("fin", i - 2)})
        pool += [("rsum", i - 2)]
    if not last:
        pool += [("split q", i + 1), ("split k", i + 1)]
        sync += [("load x", i + 2)] if not (i.a == 0 and i.c + 2 >= BATCH) else []
    sync += [("store g", i)]
    if not last:
        sync += [("stack q", i + 1), ("stack k", i + 1)]
    if not first:
        pool += [("mix", i - 2)]
    pool += [("max past 0", i - 1)]
    sync += [("max past 0", i - 1)]
    if not first:
        pool += [("gated", i - 2)]
        sync += [("store out", i - 2)]
    return Slot(("own", i), ("past", i - 1), small, pool, sync)


def even_slot(i, last=False):
    small = {1: ("ctx own 1", i), 2: ("max past 1", i - 1), 3: ("ctxT", i), 4: ("o", i), 5: ("rq", i),
             6: ("ctx past 0", i - 1), 10: ("ctx past 1", i - 1), 14: ("ctx past 2", i - 1)}
    pool = [("max past 1", i - 1), ("split rq", i)]
    sync = [("max past 1", i - 1), ("load late", i - 1), ("stack rq", i)]
    if last:
        small[13] = ("max past 0", i)
        pool += [("max past 0", i)]
        sync += [("max past 0", i)]
        plan = {b: [2 * (b - 8), 2 * (b - 8) + 1] for b in range(8, 16)}
        return Slot(("past", i - 1), ("past", i), small, pool, sync, plan=plan)
    small.update({7: ("ffn gate 0", i + 1), 8: ("ffn up 0", i + 1), 9: ("max own 0", i + 1),
                  11: ("ffn gate 1", i + 1), 12: ("ffn up 1", i + 1), 13: ("ffn gate 2", i + 1),
                  15: ("ffn up 2", i + 1)})
    pool += [("max own 0", i + 1)]
    sync += [("max own 0", i + 1)]
    stats = (11, i + 2) if not (i.a == 0 and i.c + 2 >= BATCH) else None
    return Slot(("past", i - 1), ("own", i + 1), small, pool, sync, stats)


def first_slots():
    n = lambda i: Count(0, i)
    ffn = lambda i: {3: ("ffn gate 0", n(i)), 4: ("ffn up 0", n(i)), 5: ("ffn gate 1", n(i)),
                     6: ("ffn up 1", n(i)), 7: ("ffn gate 2", n(i)), 8: ("ffn up 2", n(i))}
    project = lambda i: {0: ("xnT", n(i)), 1: ("q", n(i)), 2: ("k", n(i)), 3: ("v", n(i))}
    splits = lambda i: [("xn", n(i)), ("split q", n(i)), ("split k", n(i))]
    a = Slot(None, None, project(0), splits(0), [("load x", n(1)), ("stack q", n(0)), ("stack k", n(0))],
             stats=(0, n(0)))
    small = {**{b - 3: t for b, t in ffn(0).items()}, **{b + 6: t for b, t in project(1).items()}}
    small.update({12: ("max own 0", n(0))})
    b = Slot(None, ("own", n(0)), small, splits(1) + [("max own 0", n(0))],
             [("load x", n(2)), ("stack q", n(1)), ("stack k", n(1)), ("max own 0", n(0))], stats=(0, n(1)))
    small = {**ffn(1), **{1: ("ffn y", n(0)), 2: ("max own 1", n(0)), 9: ("max own 0", n(1)), 10: ("ctx own 0", n(0))}}
    c = Slot(("own", n(0)), ("own", n(1)), small, [("max own 1", n(0)), ("max own 0", n(1))],
             [("max own 1", n(0)), ("store g", n(0)), ("max own 0", n(1))], stats=(11, n(2)))
    d = Slot(None, None, {1: ("ctx own 1", n(0)), 3: ("ctxT", n(0)), 4: ("o", n(0)), 5: ("rq", n(0))},
             [("split rq", n(0))], [("stack rq", n(0))])
    return [a, b, c, d, odd_slot(n(1), first=True), even_slot(n(1))]


def last_slots():
    n = lambda i: Count(0, i)
    L = BATCH - 1
    a = Slot(("past", n(L)), None,
             {1: ("ctx past 3", n(L - 1)), 2: ("max past 1", n(L)), 4: ("rctxT", n(L - 1)), 5: ("gate", n(L - 1)),
              7: ("ctx past 0", n(L)), 8: ("fin", n(L - 1)), 10: ("ctx past 1", n(L)), 14: ("ctx past 2", n(L))},
             [("max past 1", n(L)), ("rsum", n(L - 1)), ("mix", n(L - 1)), ("gated", n(L - 1))],
             [("max past 1", n(L)), ("store out", n(L - 1)), ("load late", n(L))])
    b = Slot(None, None, {1: ("ctx past 3", n(L)), 3: ("rctxT", n(L)), 4: ("gate", n(L)), 5: ("fin", n(L))},
             [("rsum", n(L)), ("mix", n(L)), ("gated", n(L))], [("store out", n(L))])
    return [odd_slot(n(L - 1)), even_slot(n(L - 1)), odd_slot(n(L), last=True), even_slot(n(L), last=True), a, b]


LOOP_FIRST = 2
TURNS = (BATCH - 2 - LOOP_FIRST) // 2


def loop_slots():
    i = Count(2, LOOP_FIRST)
    return [odd_slot(i), even_slot(i), odd_slot(i + 1), even_slot(i + 1)]


def build(nc, x, past, weights, columns, rows, w_gate, w_up, w_down, out):
    with ExitStack() as ctx:
        def sb(name, shape, dt):
            return ctx.enter_context(nc.sbuf_tensor(name, shape, dt))

        def psum(name, shape, dt):
            return ctx.enter_context(nc.psum_tensor(name, shape, dt))

        def sem(name):
            return ctx.enter_context(nc.semaphore(name))

        W = sb("W", [128, 9, H], F32)
        Wq, Wk, Wv, Wo, Wrq, Wrk, Wrv, Wg_own, Wg_past = (W[:, n, :] for n in range(9))
        cols = sb("cols", [128, 6], F32)
        bq, bk, bo, brq, brk, bg = (cols[:, n:n + 1] for n in range(6))
        half_bg = sb("half_bg", [128, 1], F32)
        brows = sb("brows", [128, 2, H], F32)
        wint = sb("wint", [128, 3, HIDDEN], I32)
        wffn = sb("wffn", [128, 3, HIDDEN], F32)
        ident = sb("ident", [128, 128], F32)
        identb = sb("identb", [128, 128], BF16)
        minus_half = sb("minus_half", [128, ST], F32)
        x_in = sb("x_in", [128, ST, H], F32)
        bn = sb("bn", [128, ST, 6], F32)
        mean_var = sb("mean_var", [128, ST, 2], F32)
        var_eps = sb("var_eps", [128, ST], F32)
        rstd = sb("rstd", [128, ST], F32)
        xn = sb("xn", [128, ST, H], F32)
        xnT = sb("xnT", [128, S], F32)
        flat = {n: sb(f"flat_{n}", [128, S], F32) for n in ("q", "k", "rq")}
        rest = sb("rest", [128, S], F32)
        parts = {n: sb(f"parts_{n}", [128, PARTS, S], BF16) for n in ("q", "k", "rq")}
        stack_q = [sb(f"stack_q{p}", [128, PAIRS, S], BF16) for p in range(2)]
        stack_k = [sb(f"stack_k{p}", [128, PAIRS, S], BF16) for p in range(2)]
        stack_rq = [sb(f"stack_rq{p}", [128, PAIRS, S], BF16) for p in range(2)]
        stack_rk = sb("stack_rk", [128, PAIRS, S], BF16)
        values = [sb(f"values{p}", [128, ST, HEADS, 32], F32) for p in range(2)]
        past_values = sb("past_values", [128, ST, HEADS, 32], F32)
        MW = {"own": 1, "past": PAST}
        top = {n: sb(f"top_{n}", [128, 2, ST, 2, MW[n], PAIRS // 2], F32) for n in MW}
        top_rest = {n: sb(f"top_rest_{n}", [128, ST * 2 * MW[n], PAIRS // 2], F32) for n in MW}
        top_parts = {n: sb(f"top_parts_{n}", [128, 2, ST, 2 * MW[n], PARTS, PAIRS // 2], BF16) for n in MW}
        TR = {n: 2 * MW[n] * PARTS * (PAIRS // 2) for n in MW}
        TB = {n: 96 // TR[n] for n in MW}
        topT = {n: sb(f"topT_{n}", [96, 2, S // TB[n]], BF16) for n in MW}
        probs = sb("probs", [128, PBUF, QUAD, S], F32)
        U = sb("U", [128, 2, S], F32)
        recip = sb("recip", [128, ST, QUAD, 2], F32)
        ctx_own = sb("ctx_own", [128, ST, H], F32)
        ctx_past = sb("ctx_past", [128, PAST, ST, H], F32)
        ctx_sum = sb("ctx_sum", [128, ST, H], F32)
        ctxT = sb("ctxT", [128, S], F32)
        oT = [sb(f"oT{p}", [128, S], F32) for p in range(2)]
        rT = sb("rT", [128, S], F32)
        tanh_g = sb("tanh_g", [128, S], F32)
        diff = sb("diff", [128, S], F32)
        both = sb("both", [128, S], F32)
        mixed = sb("mixed", [128, S], F32)
        product = sb("product", [128, S], F32)
        tanh_f = sb("tanh_f", [128, S], F32)
        hg = sb("hg", [128, S], F32)
        hT = sb("hT", [128, NB, S], F32)
        g_new = sb("g_new", [128, S], F32)
        g_late = sb("g_late", [128, S], F32)
        x_late = sb("x_late", [128, ST, H], F32)
        result = sb("result", [128, ST, H], F32)

        MX = [psum(f"MX{n}", [128, S], F32) for n in range(RING)]
        SC = [psum(f"SC{n}", [128, S], F32) for n in range(RING)]
        CT = psum("CT", [128, S], F32)
        Z = psum("Z", [128, S], F32)
        Zt = Z[:, :].rearrange("p (s h) -> p s h", s=ST)
        Zb = Z[:, :].bitcast(BF16)

        parts_d = {n: nc.dram_tensor(f"parts_{n}_d", [PARTS, 128, S], BF16).ap() for n in ("q", "k", "rq")}
        top_d = {n: nc.dram_tensor(f"top_{n}_d", [2, TR[n], S], BF16).ap() for n in MW}
        g_d = nc.dram_tensor("g_d", [BATCH, 128, S], F32).ap()

        s_load = sem("s_load")
        s_ones = sem("s_ones")
        s_const = sem("s_const")
        s_pat = sem("s_pat")
        s_dq = sem("s_dq")
        past_split = sem("past_split")
        s_id = sem("s_id")
        s_past_v = sem("s_past_v")
        s_past_sb2 = sem("s_past_sb2")
        s_past_ps, s_past_sb = sem("s_past_ps"), sem("s_past_sb")
        x_loaded = sem("x_loaded")
        bn_done = sem("bn_done")
        stats_done = sem("stats_done")
        rstd_steps = sem("rstd_steps")
        xn_made = sem("xn_made")
        filled = {}
        emptied = {}
        TIMES = {"max own": 2, "max past": 2, "ctx own": 2, "ctx past": 4, "ffn gate": NB, "ffn up": NB}
        for n in ("xnT", "q", "k", "v", "max own", "max past", "ctx own", "ctx past", "ctxT", "o", "rq", "rctxT",
                  "gate", "fin", "ffn gate", "ffn up", "ffn y"):
            filled[n] = sem("filled_" + n.replace(" ", "_"))
            emptied[n] = sem("emptied_" + n.replace(" ", "_"))
        tanh_done = {n: sem("tanh_" + n.replace(" ", "_")) for n in ("ffn gate", "ffn y")}
        split_steps = {n: sem(f"split_steps_{n}") for n in ("q", "k", "rq")}
        parts_stored = {n: sem(f"parts_stored_{n}") for n in ("q", "k", "rq")}
        stacked = {n: sem(f"stacked_{n}") for n in ("q", "k", "rq")}
        max_scored = sem("max_scored")
        max_taken = sem("max_taken")
        scored = sem("scored")
        exp_done = sem("exp_done")
        beats_done = sem("beats_done")
        top_steps = {n: sem(f"top_steps_{n}") for n in MW}
        top_stored = {n: sem(f"top_stored_{n}") for n in MW}
        top_loaded = {n: sem(f"top_loaded_{n}") for n in MW}
        U_filled = {n: sem(f"U_filled_{n}") for n in MW}
        recip_done = {n: sem(f"recip_done_{n}") for n in MW}
        rsum_done = sem("rsum_done")
        mix_done = sem("mix_done")
        gated_steps = sem("gated_steps")
        g_stored = sem("g_stored")
        late_loaded = sem("late_loaded")
        out_stored = sem("out_stored")

        def order(task):
            name, _, n = task.rpartition(" ")
            return (name, int(n)) if n.isdigit() else (task, 0)

        def nth(task, i):
            name, n = order(task)
            return TIMES.get(name, 1) * i + (n + 1)

        def hold(engine, turn):
            if turn is not None:
                engine.nop(nofuse=True)

        UROUNDS = {"own": 2, "past": 4}

        def head_rows(u):
            return 64 * (u % 2)

        block = ctx.enter_context(nc.Block())

        @block.sync
        def _(sp):
            def load_x(i, t):
                if i > 0:
                    sp.wait_ge(xn_made, i.at(t))
                src = x[bass.ds(i.at(t), 1)] if t is not None else x[i.c:i.c + 1]
                sp.dma_start(x_in[:], src.rearrange("o (s p) f -> p (o s) f", p=128)).then_inc(x_loaded, 16)

            def stack_parts(dst, src, backwards, raised):
                for par in range(2):
                    v = src.rearrange("j (par d pos) s -> par j d (pos s)", par=2, pos=PAIRS)[par]
                    row = 64 * par
                    for n in (3, 2, 1):
                        take = v[PARTS - n:PARTS] if backwards else v[0:n]
                        sp.dma_start(dst[row:row + n * D].rearrange("p a b -> p (a b)"), take).then_inc(raised, 16)
                        row += n * D

            def stack_task(name, i, t, dst, kind):
                sp.wait_ge(split_steps[name], (4 * i + 4).at(t))
                if i > 0:
                    sp.wait_ge(stacked[name], (96 * i).at(t))
                sp.dma_start(parts_d[name].rearrange("j p s -> p j s"), parts[name][:]).then_inc(parts_stored[name], 16)
                sp.wait_ge(parts_stored[name], (16 * i + 16).at(t))
                if i - 1 > 0:
                    sp.wait_ge(scored, (TILES * (stage(kind, i - 2) + 1)).at(t))
                stack_parts(dst, parts_d[name], name == "k", stacked[name])

            def top_task(kind, half, i, p, t):
                sp.wait_ge(emptied[f"max {kind}"], (2 * i + (half + 1)).at(t))
                if i > 0:
                    sp.wait_ge(top_loaded[kind], (64 * i).at(t))
                tb, r = TB[kind], TR[kind]
                for m in range(tb):
                    sp.dma_start(top_d[kind][half].rearrange("r (c m q) -> m r c q", m=tb, q=128)[m],
                                 topT[kind][m * r:(m + 1) * r, half, :].rearrange("r (c q) -> r c q", q=128)
                                 ).then_inc(top_stored[kind], 16)
                sp.wait_ge(top_stored[kind], (32 * tb * i + 16 * tb * (half + 1)).at(t))
                dst = (stack_q if kind == "own" else stack_rq)[p]
                n = MW[kind] * PARTS
                for par in range(2):
                    row = 64 * par + MAXROW
                    sp.dma_start(dst[row:row + n, half * 4:half * 4 + 4, :].rearrange("p a b -> p (a b)"),
                                 top_d[kind][half].rearrange("(par j pos) s -> par j (pos s)", par=2, j=n)[par]
                                 ).then_inc(top_loaded[kind], 16)

            def task(name, i, t):
                p = i.c % 2
                if name == "load x":
                    load_x(i, t)
                elif name == "stack q":
                    stack_task("q", i, t, stack_q[p], "own")
                elif name == "stack k":
                    stack_task("k", i, t, stack_k[p], "own")
                elif name == "stack rq":
                    stack_task("rq", i, t, stack_rq[p], "past")
                elif name.startswith("max"):
                    _, kind, half = name.split()
                    top_task(kind, int(half), i, p, t)
                elif name == "store g":
                    sp.wait_ge(emptied["ffn y"], (i + 1).at(t))
                    dst = g_d[bass.ds(i.at(t), 1)] if t is not None else g_d[i.c:i.c + 1]
                    sp.dma_start(dst.rearrange("o p s -> p (o s)"), g_new[:]).then_inc(g_stored, 16)
                elif name == "load late":
                    sp.wait_ge(g_stored, (16 * i + 16).at(t))
                    if i > 0:
                        sp.wait_ge(out_stored, (16 * i).at(t))
                    src = g_d[bass.ds(i.at(t), 1)] if t is not None else g_d[i.c:i.c + 1]
                    sp.dma_start(g_late[:], src.rearrange("o p s -> p (o s)")).then_inc(late_loaded, 16)
                    src = x[bass.ds(i.at(t), 1)] if t is not None else x[i.c:i.c + 1]
                    sp.dma_start(x_late[:], src.rearrange("o (s p) f -> p (o s) f", p=128)).then_inc(late_loaded, 16)
                elif name == "store out":
                    sp.wait_ge(emptied["fin"], (i + 1).at(t))
                    dst = out[bass.ds(i.at(t), 1)] if t is not None else out[i.c:i.c + 1]
                    sp.dma_start(dst.rearrange("o (s p) f -> p (o s) f", p=128), result[:]).then_inc(out_stored, 16)

            sp.dma_start(x_in[:], x[0].rearrange("(s p) f -> p s f", p=128)).then_inc(x_loaded, 16)
            sp.dma_start(W[:], weights).then_inc(s_load, 16)
            sp.dma_start(cols[:], columns).then_inc(s_load, 16)
            sp.dma_start(brows[:], rows).then_inc(s_load, 16)
            sp.dma_start(x_late[:], past.rearrange("(s p) f -> p s f", p=128)).then_inc(s_load, 16)
            sp.dma_start(wint[:, 0, :], w_gate).then_inc(s_load, 16)
            sp.dma_start(wint[:, 1, :], w_up).then_inc(s_load, 16)
            sp.dma_start(wint[:, 2, :], w_down).then_inc(s_load, 16)
            sp.wait_ge(s_ones, 6)
            pattern = probs[0:3, 0:2].rearrange("p a b c -> p (a b c)").bitcast(BF16)
            for par in range(2):
                for n in range(PAST):
                    row = 64 * par + MAXROW + n * PARTS
                    sp.dma_start(stack_rk[row:row + PARTS].rearrange("p a b -> p (a b)"),
                                 pattern[:, n * PAIRS * S:(n + 1) * PAIRS * S]).then_inc(s_pat, 16)
            sp.wait_ge(past_split, 4)
            sp.dma_start(parts_d["k"].rearrange("j p s -> p j s"), parts["k"][:]).then_inc(s_pat, 16)
            sp.wait_ge(s_pat, 80)
            stack_parts(stack_rk, parts_d["k"], True, s_pat)
            sp.wait_ge(s_pat, 80 + 96)

            for slot in first_slots():
                for name, i in slot.sync:
                    task(name, i, None)
            with sp.Fori(0, TURNS) as turn:
                for slot in loop_slots():
                    for name, i in slot.sync:
                        task(name, i, turn)
            for slot in last_slots():
                for name, i in slot.sync:
                    task(name, i, None)
            sp.wait_ge(out_stored, 16 * BATCH)
            sp.wait_ge(g_stored, 16 * BATCH)

        @block.tensor
        def _(pe):
            def free_Z(before, t):
                if before:
                    name, i = before
                    pe.wait_ge(emptied[order(name)[0]], nth(name, i).at(t))

            def transposes(dst, src, n_last):
                for st in range(ST):
                    last = nc.tensor.transpose(dst[:, st * 128:(st + 1) * 128], src[:, st, :], ident[:])
                return last

            def small_task(name, i, before, t):
                kind, n = order(name)
                p = i.c % 2
                done = filled[kind]
                if kind == "xnT":
                    pe.wait_ge(xn_made, (i + 1).at(t))
                elif kind in ("q", "k", "v"):
                    pe.wait_ge(emptied["xnT"], (i + 1).at(t))
                elif kind in ("max own", "max past"):
                    pe.wait_ge(top_steps[kind[4:]], (8 * i + 4 * (n + 1)).at(t))
                elif kind in ("ctx own", "ctx past"):
                    pe.wait_ge(U_filled[kind[4:]], nth(name, i).at(t))
                elif kind == "ctxT":
                    pe.wait_ge(emptied["ctx own"], (2 * i + 2).at(t))
                elif kind == "o":
                    pe.wait_ge(emptied["ctxT"], (i + 1).at(t))
                elif kind == "rq":
                    pe.wait_ge(emptied["o"], (i + 1).at(t))
                elif kind == "rctxT":
                    pe.wait_ge(rsum_done, (i + 1).at(t))
                elif kind == "gate":
                    pe.wait_ge(emptied["rctxT"], (i + 1).at(t))
                elif kind == "fin":
                    pe.wait_ge(gated_steps, (3 * i + 3).at(t))
                elif kind == "ffn gate":
                    pe.wait_ge(emptied["xnT"], (i + 1).at(t))
                elif kind == "ffn up":
                    pe.wait_ge(emptied["ffn gate"], nth("ffn gate %d" % n, i).at(t))
                elif kind == "ffn y":
                    pe.wait_ge(emptied["ffn up"], (NB * i + NB).at(t))
                free_Z(before, t)
                if kind == "xnT":
                    last = transposes(Z, xn, None)
                elif kind == "q":
                    last = nc.tensor.matmul(Z[:], Wq, xnT[:], start=True, stop=True)
                elif kind == "k":
                    last = nc.tensor.matmul(Z[:], Wk, xnT[:], start=True, stop=True)
                elif kind == "v":
                    for st in range(ST):
                        last = nc.tensor.matmul(Z[:, st * H:(st + 1) * H], xnT[:, st * 128:(st + 1) * 128], Wv,
                                                start=True, stop=True)
                elif kind in ("max own", "max past"):
                    tb = TB[kind[4:]]
                    for c in range(ST // tb):
                        last = nc.tensor.transpose(
                            Zb[0:96, c * 128:(c + 1) * 128],
                            top_parts[kind[4:]][:, n, c * tb:(c + 1) * tb].rearrange("p s m j c -> p (s m j c)"), identb[:])
                elif kind in ("ctx own", "ctx past"):
                    src = U[:, n % 2, :].rearrange("p (s q) -> p s q", s=ST)
                    last = transposes(Z, src, None)
                elif kind == "ctxT":
                    last = transposes(Z, ctx_own, None)
                elif kind == "o":
                    last = nc.tensor.matmul(Z[:], Wo, ctxT[:], start=True, stop=True)
                elif kind == "rq":
                    last = nc.tensor.matmul(Z[:], Wrq, oT[p][:], start=True, stop=True)
                elif kind == "rctxT":
                    last = transposes(Z, ctx_sum, None)
                elif kind == "gate":
                    nc.tensor.matmul(Z[:], Wg_own, oT[p][:], start=True, stop=False)
                    last = nc.tensor.matmul(Z[:], Wg_past, rT[:], start=False, stop=True)
                elif kind == "fin":
                    last = transposes(Z, product[:].rearrange("p (s q) -> p s q", s=ST), None)
                elif kind == "ffn gate":
                    last = nc.tensor.matmul(Z[:], wffn[:, 0, n * 128:(n + 1) * 128], xnT[:], start=True, stop=True)
                elif kind == "ffn up":
                    last = nc.tensor.matmul(Z[:], wffn[:, 1, n * 128:(n + 1) * 128], xnT[:], start=True, stop=True)
                elif kind == "ffn y":
                    for b in range(NB):
                        last = nc.tensor.matmul(Z[:], wffn[:, 2, b * 128:(b + 1) * 128], hT[:, b, :],
                                                start=(b == 0), stop=(b == NB - 1))
                last.then_inc(done, 1)

            def maxima_tile(kind, i, s, beat, u, t):
                group, st = divmod(beat, ST)
                pos, row = 2 * group + u // 2, head_rows(u)
                n = 4 * beat + u
                qs, ks = (stack_q[i.c % 2], stack_k[i.c % 2]) if kind == "own" else (stack_rq[i.c % 2], stack_rk)
                if n == 0:
                    if kind == "own":
                        pe.wait_ge(stacked["q"], (96 * i + 96).at(t))
                        pe.wait_ge(stacked["k"], (96 * i + 96).at(t))
                    else:
                        pe.wait_ge(stacked["rq"], (96 * i + 96).at(t))
                if in_ring(s, n) > 0:
                    pe.wait_ge(max_taken, in_ring(s, n).at(t))
                nc.tensor.matmul(MX[n % RING][:], qs[row:row + ROWS, pos, st * 128:(st + 1) * 128],
                                 ks[row:row + ROWS, pos, :], start=True, stop=True).then_inc(max_scored, 1)

            def score_tile(kind, i, s, beat, u, t):
                group, st = divmod(beat, ST)
                pos, row = 2 * group + u // 2, head_rows(u)
                n = 4 * beat + u
                k_rows = ROWS + PARTS * MW[kind]
                qs, ks = (stack_q[i.c % 2], stack_k[i.c % 2]) if kind == "own" else (stack_rq[i.c % 2], stack_rk)
                if n == 0:
                    pe.wait_ge(top_loaded[kind], (64 * i + 32).at(t))
                if n == TILES // 2:
                    pe.wait_ge(top_loaded[kind], (64 * i + 64).at(t))
                if in_ring(s, n) > 0:
                    pe.wait_ge(exp_done, in_ring(s, n).at(t))
                nc.tensor.matmul(SC[n % RING][:], ks[row:row + k_rows, pos, st * 128:(st + 1) * 128],
                                 qs[row:row + k_rows, pos, :], start=True, stop=True).then_inc(scored, 1)

            def weigh_values(kind, i, s, beat, U_before, t):
                group, st = divmod(beat, ST)
                vals = values[i.c % 2] if kind == "own" else past_values
                per = ST * GROUPS // UROUNDS[kind]
                pe.wait_ge(exp_done, (TILES * s + 4 * (beat + 1)).at(t))
                if beat == 0 and kind == "own":
                    pe.wait_ge(emptied["v"], (i + 1).at(t))
                if beat % per == 0 and U_before:
                    k0, v0 = U_before
                    pe.wait_ge(U_filled[k0], v0.at(t))
                for u in range(QUAD):
                    last = nc.tensor.matmul(CT[32 * u:32 * u + 32, :], vals[:, st, FIRST_HEAD[group] + u, :],
                                            probs[:, beat % PBUF, u, :], start=(beat % per == 0),
                                            stop=(beat % per == per - 1), skip_group_check=True)
                last.then_inc(beats_done, 1)

            def run(slots, before, pending, U_before, t):
                for slot in slots:
                    E, M = slot.probs, slot.maxima
                    for b in range(BEATS):
                        tiles = [(mb, u) for mb in (slot.plan.get(b, []) if M else []) for u in range(QUAD)]
                        if M:
                            sM = stage(*M)
                        for mb, u in tiles[:len(tiles) // 2]:
                            maxima_tile(*M, sM, mb, u, t)
                        if E:
                            for u in (0, 1):
                                score_tile(*E, stage(*E), b, u, t)
                        if pending:
                            kind, i, beat = pending
                            s = stage(kind, i)
                            weigh_values(kind, i, s, beat, U_before, t)
                            per = BEATS // UROUNDS[kind]
                            if beat % per == per - 1:
                                U_before = (kind, UROUNDS[kind] * i + (beat // per + 1))
                        for mb, u in tiles[len(tiles) // 2:]:
                            maxima_tile(*M, sM, mb, u, t)
                        if E:
                            for u in (2, 3):
                                score_tile(*E, stage(*E), b, u, t)
                        if b in slot.small:
                            name, i = slot.small[b]
                            small_task(name, i, before, t)
                            before = (name, i)
                        pending = (*E, b) if E else None
                return before, pending, U_before

            pe.wait_ge(s_load, 16 * 7)
            pe.wait_ge(s_id, 2)
            transposes(Z, x_late, None).then_inc(s_past_ps, 1)
            pe.wait_ge(s_past_sb, 1)
            nc.tensor.matmul(Z[:], Wrk, xnT[:], start=True, stop=True).then_inc(s_past_ps, 1)
            pe.wait_ge(s_past_sb, 2)
            for st in range(ST):
                last = nc.tensor.matmul(Z[:, st * H:(st + 1) * H], xnT[:, st * 128:(st + 1) * 128], Wrv,
                                        start=True, stop=True)
            last.then_inc(s_past_ps, 1)
            pe.wait_ge(s_past_v, 2)
            pe.wait_ge(s_pat, 80 + 96)
            pe.wait_ge(s_dq, 4)

            before, pending, U_before = run(first_slots(), None, None, None, None)
            i = Count(2, LOOP_FIRST)
            with pe.Fori(0, TURNS) as turn:
                run(loop_slots(), (before[0], i), ("past", i - 2, BEATS - 1), ("past", 4 * (i - 2) + 3), turn)
            i = Count(0, LOOP_FIRST + 2 * TURNS)
            run(last_slots(), (before[0], i), ("past", i - 2, BEATS - 1), ("past", 4 * (i - 2) + 3), None)

        @block.scalar
        def _(act):
            def probabilities(kind, i, s, beat, u, t):
                n = 4 * beat + u
                act.wait_ge(scored, (TILES * s + (n + 1)).at(t))
                if u == 0 and BEATS * s + (beat - PBUF + 1) > 0:
                    act.wait_ge(beats_done, (BEATS * s + (beat - PBUF + 1)).at(t))
                nc.scalar.activation(probs[:, beat % PBUF, u, :], SC[n % RING][:], ACT.Exp,
                                     scale=SCALE).then_inc(exp_done, 1)

            def take_contexts(kind, i, s, beat, t):
                n = beat // (BEATS // UROUNDS[kind])
                act.wait_ge(beats_done, (BEATS * s + (beat + 1)).at(t))
                nc.scalar.activation(U[:, n % 2, :], CT[:], ACT.Copy).then_inc(U_filled[kind], 1)

            def small_task(name, i, t):
                kind, n = order(name)
                p = i.c % 2
                if kind in ("v", "ctx own", "ctx past", "fin", "ffn up"):
                    return
                act.wait_ge(filled[kind], nth(name, i).at(t))
                if kind == "xnT":
                    nc.scalar.activation(xnT[:], Z[:], ACT.Copy).then_inc(emptied[kind], 1)
                elif kind in ("q", "k", "rq"):
                    if i > 0:
                        act.wait_ge(split_steps[kind], (4 * i).at(t))
                    nc.scalar.activation(flat[kind][:], Z[:], ACT.Identity,
                                         bias={"q": bq, "k": bk, "rq": brq}[kind]).then_inc(emptied[kind], 1)
                elif kind in ("max own", "max past"):
                    nc.scalar.activation(topT[kind[4:]][:, n, :], Zb[0:96, 0:S // TB[kind[4:]]],
                                         ACT.Copy).then_inc(emptied[kind], 1)
                elif kind == "ctxT":
                    nc.scalar.activation(ctxT[:], Z[:], ACT.Copy).then_inc(emptied[kind], 1)
                elif kind == "o":
                    nc.scalar.activation(oT[p][:], Z[:], ACT.Identity, bias=bo).then_inc(emptied[kind], 1)
                elif kind == "rctxT":
                    nc.scalar.activation(rT[:], Z[:], ACT.Copy, scale=1.0 / PAST).then_inc(emptied[kind], 1)
                elif kind == "gate":
                    nc.scalar.activation(tanh_g[:], Z[:], ACT.Tanh, bias=half_bg[:], scale=0.5).then_inc(emptied[kind], 1)
                elif kind in ("ffn gate", "ffn y"):
                    nc.scalar.activation(tanh_f[:], Z[:], ACT.Tanh, scale=0.5).then_inc(tanh_done[kind], 1)

            def run(slots, pending, t):
                for slot in slots:
                    E = slot.probs
                    for b in range(BEATS):
                        if E:
                            for u in (0, 1):
                                probabilities(*E, stage(*E), b, u, t)
                        if pending:
                            kind, i, beat = pending
                            per = BEATS // UROUNDS[kind]
                            if beat % per == per - 1:
                                take_contexts(kind, i, stage(kind, i), beat, t)
                        if E:
                            for u in (2, 3):
                                probabilities(*E, stage(*E), b, u, t)
                        if b in slot.small:
                            small_task(*slot.small[b], t)
                        pending = (*E, b) if E else None

            act.wait_ge(s_load, 16 * 7)
            nc.scalar.activation(half_bg[:], bg, ACT.Copy, scale=0.5).then_inc(s_past_sb2, 1)
            act.wait_ge(s_past_ps, 1)
            nc.scalar.activation(xnT[:], Z[:], ACT.Copy).then_inc(s_past_sb, 1)
            act.wait_ge(s_past_ps, 2)
            nc.scalar.activation(flat["k"][:], Z[:], ACT.Identity, bias=brk).then_inc(s_past_sb, 1)
            act.wait_ge(past_split, 4)
            act.wait_ge(s_past_sb2, 1)

            run(first_slots(), None, None)
            i = Count(2, LOOP_FIRST)
            with act.Fori(0, TURNS) as turn:
                run(loop_slots(), ("past", i - 2, BEATS - 1), turn)
            run(last_slots(), ("past", Count(0, LOOP_FIRST + 2 * TURNS - 2), BEATS - 1), None)

        @block.vector
        def _(dve):
            def take_maxima(kind, i, s, beat, u, t):
                group, st = divmod(beat, ST)
                pos, par, n = 2 * group + u // 2, u % 2, 4 * beat + u
                half, c = divmod(pos, PAIRS // 2)
                if n % (TILES // 2) == 0 and i > 0:
                    dve.wait_ge(top_steps[kind], (8 * i - (4 if n == 0 else 0)).at(t))
                dve.wait_ge(max_scored, (TILES * s + (n + 1)).at(t))
                nc.vector.tensor_reduce(top[kind][:, half, st, par, :, c],
                                        MX[n % RING][:].rearrange("p (w k) -> p w k", w=MW[kind]),
                                        AX_X, ALU.max, negate=True).then_inc(max_taken, 1)

            def small_task(name, i, t):
                kind, n = order(name)
                if kind == "v":
                    dve.wait_ge(filled[kind], (i + 1).at(t))
                    if i - 1 > 0:
                        dve.wait_ge(beats_done, (BEATS * (stage("own", i - 2) + 1)).at(t))
                    for a in range(2):
                        last = nc.vector.tensor_tensor(
                            values[i.c % 2][:, :, 8 * a:8 * a + 8, SLOT * a:SLOT * a + D],
                            Zt[:, :, 64 * a:64 * a + 64].rearrange("p s (h d) -> p s h d", d=D),
                            brows[:, 0:1, 64 * a:64 * a + 64].rearrange("p o (h d) -> p o h d", d=D).to_broadcast([128, ST, 8, D]),
                            ALU.add)
                    last.then_inc(emptied[kind], 1)
                elif kind in ("ctx own", "ctx past"):
                    k2 = kind[4:]
                    dve.wait_ge(filled[kind], nth(name, i).at(t))
                    if k2 == "past" and n == 0 and i > 0:
                        dve.wait_ge(rsum_done, i.at(t))
                    zc = Z[:].rearrange("p (s q c) -> p s q c", s=ST, q=QUAD)
                    nc.vector.reciprocal(recip[:], zc[:, :, :, D:D + SLOT + 1:SLOT]).then_inc(recip_done[k2], 1)
                    dve.wait_ge(recip_done[k2], nth(name, i).at(t))
                    for a in range(2):
                        if k2 == "own":
                            c0 = (FIRST_HEAD[2 * n + a]) * D
                            dst = ctx_own[:, :, c0:c0 + QUAD * D]
                        else:
                            c0 = FIRST_HEAD[n] * D
                            dst = ctx_past[:, a, :, c0:c0 + QUAD * D]
                        last = nc.vector.tensor_tensor(dst.rearrange("p s (q d) -> p s q d", d=D),
                                                       zc[:, :, :, SLOT * a:SLOT * a + D],
                                                       recip[:, :, :, a:a + 1].to_broadcast([128, ST, QUAD, D]), ALU.mult)
                    last.then_inc(emptied[kind], 1)
                elif kind == "fin":
                    dve.wait_ge(filled[kind], (i + 1).at(t))
                    dve.wait_ge(late_loaded, (32 * i + 32).at(t))
                    nc.vector.scalar_tensor_tensor(out=result[:], in0=Zt, scalar=0.25, in1=x_late[:],
                                                   op0=ALU.mult, op1=ALU.add).then_inc(emptied[kind], 1)
                elif kind == "ffn gate":
                    dve.wait_ge(tanh_done[kind], nth(name, i).at(t))
                    nc.vector.scalar_tensor_tensor(out=hg[:], in0=tanh_f[:], scalar=1.0, in1=Z[:],
                                                   op0=ALU.add, op1=ALU.mult).then_inc(emptied[kind], 1)
                elif kind == "ffn up":
                    dve.wait_ge(filled[kind], nth(name, i).at(t))
                    nc.vector.tensor_tensor(hT[:, n, :], hg[:], Z[:], ALU.mult).then_inc(emptied[kind], 1)
                elif kind == "ffn y":
                    dve.wait_ge(tanh_done[kind], (i + 1).at(t))
                    if i > 0:
                        dve.wait_ge(g_stored, (16 * i).at(t))
                    nc.vector.scalar_tensor_tensor(out=g_new[:], in0=tanh_f[:], scalar=1.0, in1=Z[:],
                                                   op0=ALU.add, op1=ALU.mult).then_inc(emptied[kind], 1)

            def statistics(i, t):
                dve.wait_ge(x_loaded, (16 * i + 16).at(t))
                for st in range(ST):
                    last = nc.vector.bn_stats(bn[:, st, :], x_in[:, st, :])
                last.then_inc(bn_done, 1)
                dve.wait_ge(bn_done, (i + 1).at(t))
                if i > 0:
                    dve.wait_ge(xn_made, i.at(t))
                hold(dve, t)
                for st in range(ST):
                    last = nc.vector.bn_aggr(mean_var[:, st, :], bn[:, st, :])
                last.then_inc(stats_done, 1)

            def run(slots, late, t):
                for slot in slots:
                    M = slot.maxima
                    for b in range(BEATS):
                        tiles = [(mb, u) for mb in (slot.plan.get(b, []) if M else []) for u in range(QUAD)]
                        for mb, u in tiles[:len(tiles) // 2]:
                            take_maxima(*M, stage(*M), mb, u, t)
                        if slot.stats and slot.stats[0] == b:
                            statistics(slot.stats[1], t)
                        if late:
                            small_task(*late, t)
                        for mb, u in tiles[len(tiles) // 2:]:
                            take_maxima(*M, stage(*M), mb, u, t)
                        late = slot.small.get(b)
                return late

            for v in (values[0], values[1], past_values):
                last = nc.vector.memset(v[:], 0.0)
            last.then_inc(s_ones, 1)
            for k in (stack_k[0], stack_k[1]):
                for row in (32, 96):
                    nc.vector.memset(k[row:row + 32], 1.0)
            pattern = probs[0:3, 0:2].rearrange("p a b c -> p (a b c)").bitcast(BF16).rearrange(
                "p (n a w k) -> p n a w k", n=PAST, a=PAIRS, w=PAST)
            nc.vector.memset(pattern[:, 0, :, 0, :], 1.0).then_inc(s_ones, 1)
            nc.vector.memset(pattern[:, 0, :, 1, :], 0.0).then_inc(s_ones, 1)
            nc.vector.memset(pattern[:, 1, :, 0, :], 0.0).then_inc(s_ones, 1)
            nc.vector.memset(pattern[:, 1, :, 1, :], 1.0).then_inc(s_ones, 1)
            dve.wait_ge(s_ones, 1)
            for a in range(2):
                for v in (values[0], values[1]):
                    nc.vector.memset(v[:, :, 8 * a:8 * a + 8, SLOT * a + D:SLOT * a + D + 1], 1.0)
                last = nc.vector.memset(past_values[:, 2 * a:2 * a + 2, :, SLOT * a + D:SLOT * a + D + 1], 1.0)
            last.then_inc(s_ones, 1)
            dve.wait_ge(s_load, 16 * 7)
            for n in range(2):
                nc.vector.tensor_scalar(wffn[:, n, :], wint[:, n, :], DEQUANT, None, ALU.mult).then_inc(s_dq, 1)
            nc.vector.tensor_scalar(wffn[:, 2, :], wint[:, 2, :], DEQUANT, 0.5, ALU.mult, ALU.mult).then_inc(s_dq, 1)
            dve.wait_ge(s_id, 2)
            nc.vector.tensor_copy(identb[:], ident[:]).then_inc(s_dq, 1)
            dve.wait_ge(s_past_ps, 3)
            for a in range(2):
                nc.vector.tensor_tensor(
                    past_values[:, 2 * a:2 * a + 2, :, SLOT * a:SLOT * a + D],
                    Zt[:, 2 * a:2 * a + 2, :].rearrange("p s (h d) -> p s h d", d=D),
                    brows[:, 1:2, :].rearrange("p o (h d) -> p o h d", d=D).to_broadcast([128, 2, HEADS, D]),
                    ALU.add).then_inc(s_past_v, 1)

            late = run(first_slots(), None, None)
            i = Count(2, LOOP_FIRST)
            with dve.Fori(0, TURNS) as turn:
                run(loop_slots(), (late[0], i), turn)
            run(last_slots(), (late[0], Count(0, LOOP_FIRST + 2 * TURNS)), None)

        @block.gpsimd
        def _(pool):
            def split(src, res, out_parts, raised, base, t):
                hold(pool, t)
                nc.gpsimd.tensor_copy(out_parts[0], src).then_inc(raised, 1)
                pool.wait_ge(raised, (base + 1).at(t))
                nc.gpsimd.tensor_tensor(res, src, out_parts[0], ALU.subtract).then_inc(raised, 1)
                pool.wait_ge(raised, (base + 2).at(t))
                hold(pool, t)
                nc.gpsimd.tensor_copy(out_parts[1], res).then_inc(raised, 1)
                pool.wait_ge(raised, (base + 3).at(t))
                nc.gpsimd.tensor_tensor(out_parts[2], res, out_parts[1], ALU.subtract).then_inc(raised, 1)

            def top_split(kind, half, i, t):
                s = stage(kind, i)
                src = top[kind][:, half].rearrange("p s r w c -> p (s r w) c")
                dst = top_parts[kind][:, half].rearrange("p s m j c -> p (s m) j c")
                if i > 0:
                    pool.wait_ge(filled[f"max {kind}"], (2 * i + (half - 1)).at(t))
                pool.wait_ge(max_taken, (TILES * s + TILES // 2 * (half + 1)).at(t))
                split(src, top_rest[kind][:], [dst[:, :, j, :] for j in range(PARTS)],
                      top_steps[kind], 8 * i + 4 * half, t)

            def task(name, i, t):
                p = i.c % 2
                if name.startswith("max"):
                    _, kind, half = name.split()
                    top_split(kind, int(half), i, t)
                elif name.startswith("split"):
                    n = name.split()[1]
                    if i > 0:
                        pool.wait_ge(parts_stored[n], (16 * i).at(t))
                    pool.wait_ge(emptied[n], (i + 1).at(t))
                    split(flat[n][:], rest[:], [parts[n][:, j, :] for j in
                                                (range(PARTS) if n != "k" else reversed(range(PARTS)))],
                          split_steps[n], 4 * i, t)
                elif name == "xn":
                    pool.wait_ge(stats_done, (i + 1).at(t))
                    hold(pool, t)
                    nc.gpsimd.tensor_scalar(var_eps[:], mean_var[:, :, 1], EPS, None, ALU.add).then_inc(rstd_steps, 1)
                    pool.wait_ge(rstd_steps, (2 * i + 1).at(t))
                    nc.gpsimd.tensor_tensor(rstd[:], var_eps[:], minus_half[:], ALU.pow).then_inc(rstd_steps, 1)
                    if i > 0:
                        pool.wait_ge(filled["xnT"], i.at(t))
                    pool.wait_ge(rstd_steps, (2 * i + 2).at(t))
                    hold(pool, t)
                    for st in range(ST):
                        last = nc.gpsimd.tensor_scalar(xn[:, st, :], x_in[:, st, :], mean_var[:, st, 0:1],
                                                       rstd[:, st:st + 1], ALU.subtract, ALU.mult)
                    last.then_inc(xn_made, 1)
                elif name == "rsum":
                    pool.wait_ge(emptied["ctx past"], (4 * i + 4).at(t))
                    nc.gpsimd.tensor_tensor(ctx_sum[:], ctx_past[:, 0], ctx_past[:, 1], ALU.add).then_inc(rsum_done, 1)
                elif name == "mix":
                    pool.wait_ge(emptied["rctxT"], (i + 1).at(t))
                    nc.gpsimd.tensor_tensor(diff[:], rT[:], oT[p][:], ALU.subtract).then_inc(mix_done, 1)
                    nc.gpsimd.tensor_tensor(both[:], rT[:], oT[p][:], ALU.add).then_inc(mix_done, 1)
                elif name == "gated":
                    pool.wait_ge(mix_done, (2 * i + 2).at(t))
                    pool.wait_ge(emptied["gate"], (i + 1).at(t))
                    nc.gpsimd.tensor_tensor(mixed[:], tanh_g[:], diff[:], ALU.mult).then_inc(gated_steps, 1)
                    pool.wait_ge(gated_steps, (3 * i + 1).at(t))
                    nc.gpsimd.tensor_tensor(mixed[:], mixed[:], both[:], ALU.add).then_inc(gated_steps, 1)
                    pool.wait_ge(late_loaded, (32 * i + 32).at(t))
                    pool.wait_ge(gated_steps, (3 * i + 2).at(t))
                    nc.gpsimd.tensor_tensor(product[:], mixed[:], g_late[:], ALU.mult).then_inc(gated_steps, 1)

            nc.gpsimd.memset(ident[:], 0.0).then_inc(s_id, 1)
            nc.gpsimd.memset(minus_half[:], -0.5).then_inc(s_const, 1)
            pool.wait_ge(s_id, 1)
            nc.gpsimd.affine_select(out=ident[:], in_=ident[:], compare_op=ALU.not_equal, fill=1.0, base=0,
                                    pattern=[[-1, 128]], channel_multiplier=1).then_inc(s_id, 1)
            pool.wait_ge(s_const, 1)
            pool.wait_ge(s_past_sb, 2)
            split(flat["k"][:], rest[:], [parts["k"][:, j, :] for j in reversed(range(PARTS))], past_split, Count(0, 0), None)

            for slot in first_slots():
                for name, i in slot.pool:
                    task(name, i, None)
            with pool.Fori(0, TURNS) as turn:
                for slot in loop_slots():
                    for name, i in slot.pool:
                        task(name, i, turn)
            for slot in last_slots():
                for name, i in slot.pool:
                    task(name, i, None)
    return nc


def kernel(**inputs):
    import numpy as np
    import concourse.bacc as bacc
    from concourse.bass_utils import run_bass_kernel_spmd

    a = {n.removeprefix("L0_"): np.asarray(v) for n, v in inputs.items()}
    order = []
    for par in range(2):
        for d in range(D):
            for pos in range(PAIRS):
                head = FIRST_HEAD[pos // 2] + 2 * (pos % 2) + par
                order.append(head * D + d)
    order = np.array(order)
    gate = a["attn_Wg"]
    weights = np.stack([a["attn_Wq"][:, order], a["attn_Wk"][:, order], a["attn_Wv"], a["attn_Wo"],
                        a["attn_Wrq"][:, order], a["attn_Wrk"][:, order], a["attn_Wrv"], gate[:H], gate[H:]], axis=1)
    columns = np.stack([a["attn_bq"][order], a["attn_bk"][order], a["attn_bo"], a["attn_brq"][order],
                        a["attn_brk"][order], a["attn_bg"]], axis=1)
    rows = np.broadcast_to(np.stack([a["attn_bv"], a["attn_brv"]])[None], (128, 2, H))
    down = a["ffn_w_down"].T.reshape(NB, 128, H).transpose(1, 0, 2).reshape(128, NB * H)
    arrays = {
        "x": a["attn_hidden_states"], "past": a["attn_past_states"].reshape(S, H), "weights": weights,
        "columns": columns, "rows": rows, "w_gate": a["ffn_w_gate"].T, "w_up": a["ffn_w_up"].T, "w_down": down,
    }
    arrays = {n: np.ascontiguousarray(v) for n, v in arrays.items()}
    nc = bacc.Bacc("TRN2", target_bir_lowering=False, num_devices=1)
    nc.disable_value_cache = True
    args = [nc.dram_tensor(n, v.shape, mybir.dt.from_np(v.dtype), kind="ExternalInput").ap() for n, v in arrays.items()]
    out = nc.dram_tensor("out", (BATCH, S, H), F32, kind="ExternalOutput").ap()
    build(nc, *args, out)
    r = run_bass_kernel_spmd(nc, [arrays], core_ids=[0])
    return r.results[0]["out"]
```

```python
from contextlib import ExitStack

import concourse.bass as bass
from concourse import mybir

F32 = mybir.dt.float32
BF16 = mybir.dt.bfloat16
I32 = mybir.dt.int32
ALU = mybir.AluOpType
ACT = mybir.ActivationFunctionType
AX_X = mybir.AxisListType.X

BATCH = 16
S = 512
H = 128
HEADS = 16
D = H // HEADS
PAST = 2
HIDDEN = 384
NB = HIDDEN // 128
ST = S // 128
SCALE = 1.0 / float(D) ** 0.5
DEQUANT = 0.007874015718698502
EPS = 1e-5

PARTS = 3
ROWS = 6 * D
MAXROW = ROWS
STACK = 64
QUAD = 4
GROUPS = HEADS // QUAD
FIRST_HEAD = [0, 8, 4, 12]
PAIRS = HEADS // 2
BEATS = GROUPS * ST
TILES = QUAD * BEATS
RING = 3
LAG = 4
PBUF = 4
SLOT = D + 1



class Count:

    def __init__(self, a, c):
        self.a, self.c = a, c

    def __add__(self, n):
        return Count(self.a, self.c + n)

    def __sub__(self, n):
        return Count(self.a, self.c - n)

    def __mul__(self, n):
        return Count(self.a * n, self.c * n)

    __rmul__ = __mul__

    def __gt__(self, n):
        assert not (self.c <= n and self.a > 0), "zero in the first turn"
        return self.c > n

    def at(self, turn):
        return self.c if turn is None else turn * self.a + self.c


def stage(kind, i):
    n = i.c if i.a == 0 else None
    if kind == "own":
        return Count(0, n) if n in (0, 1, 2) else Count(0, 2 * n - 2) if n == BATCH - 1 else 2 * i - 1
    if n == 0 or n == BATCH - 3:
        return Count(0, 2 * n + 3)
    return Count(0, 2 * n + 1) if n == BATCH - 1 else 2 * i + 2


def rq_buffer(i):
    return 2 if i.a == 0 and i.c == BATCH - 1 else i.c % 2


def o_buffer(i):
    return 2 if i.a == 0 and i.c in (0, BATCH - 1) else i.c % 2


def in_ring(s, t):
    return TILES * s + (t - (RING - 1) if t >= RING else (0, -2, -1)[t])


class Slot:

    def __init__(self, probs, maxima, small, pool, sync, stats=None):
        self.probs, self.maxima, self.small = probs, maxima, small
        self.pool, self.sync, self.stats = pool, sync, stats

    def maxima_of(self, b):
        if self.probs is None:
            return (self.maxima, b) if self.maxima and b < BEATS - LAG else None
        if b < LAG:
            return self.probs, BEATS - LAG + b
        return (self.maxima, b - LAG) if self.maxima else None


def odd_slot(i):
    small = {1: ("ctx past 3", i - 2), 2: ("xnT", i + 1), 3: ("q", i + 1), 4: ("k", i + 1), 5: ("max own 1", i),
             6: ("ffn y", i), 7: ("rctxT", i - 2), 8: ("v", i + 1), 9: ("gate", i - 2), 10: ("ctx own 0", i),
             12: ("fin", i - 2), 13: ("max past 0", i - 1)}
    pool = [("rsum", i - 2), ("max own 1", i), ("split q", i + 1), ("split k", i + 1), ("mix", i - 2),
            ("gated", i - 2), ("max past 0", i - 1)]
    sync = [("load x", i + 2), ("max own 1", i), ("store g", i), ("stack q", i + 1), ("stack k", i + 1),
            ("store out", i - 2), ("max past 0", i - 1)]
    return Slot(("own", i), ("past", i - 1), small, pool, sync)


def even_slot(i):
    small = {1: ("ctx own 1", i), 2: ("ffn gate 0", i + 1), 3: ("ctxT", i), 4: ("o", i), 5: ("max past 1", i - 1),
             6: ("ctx past 0", i - 1), 7: ("rq", i), 8: ("ffn up 0", i + 1), 9: ("ffn gate 1", i + 1),
             10: ("ctx past 1", i - 1), 11: ("ffn up 1", i + 1), 12: ("ffn gate 2", i + 1),
             13: ("max own 0", i + 1), 14: ("ctx past 2", i - 1), 15: ("ffn up 2", i + 1)}
    pool = [("max past 1", i - 1), ("split rq", i), ("max own 0", i + 1), ("xn", i + 2)]
    sync = [("load late", i - 1), ("max past 1", i - 1), ("stack rq", i), ("max own 0", i + 1)]
    return Slot(("past", i - 1), ("own", i + 1), small, pool, sync, stats=(1, i + 2))


def numbered(*tasks):
    return {b: (name, Count(0, i)) for i, beats in tasks for b, name in beats.items()}


def listed(*tasks):
    return [(name, Count(0, i)) for name, i in tasks]


def ffn(*beats):
    return dict(zip(beats, ("ffn gate 0", "ffn up 0", "ffn gate 1", "ffn up 1", "ffn gate 2", "ffn up 2")))


CTX_PAST = {6: "ctx past 0", 10: "ctx past 1", 14: "ctx past 2"}


def first_slots():
    n = lambda i: Count(0, i)
    return [
        Slot(None, None,
             numbered((0, {0: "xnT", 1: "q", 2: "k", 3: "v", 4: "past T", 5: "past k", 6: "past v", **ffn(7, 8)})),
             listed(("xn", 0), ("xn", 1), ("split past", 0)),
             listed(("load x", 1), ("stack q", 0), ("stack k", 0), ("stack past", 0)), stats=(3, n(1))),
        Slot(None, ("own", n(0)),
             numbered((0, {0: "ffn gate 1", 1: "ffn up 1", 2: "ffn gate 2", 3: "ffn up 2", 4: "ffn y", 10: "max own 0"}),
                      (1, {5: "xnT", 6: "q", 7: "k", 8: "v", **ffn(9, 11)})),
             listed(("split q", 1), ("max own 0", 0), ("split k", 1), ("xn", 2)),
             listed(("load x", 2), ("store g", 0), ("stack q", 1), ("max own 0", 0), ("stack k", 1)), stats=(8, n(2))),
        Slot(("own", n(0)), ("own", n(1)),
             numbered((0, {5: "max own 1", 10: "ctx own 0"}),
                      (1, {0: "ffn gate 1", 1: "ffn up 1", 2: "ffn gate 2", 3: "ffn up 2", 4: "ffn y", 13: "max own 0"}),
                      (2, {6: "xnT", 7: "q", 8: "k", **ffn(9, 11, 12, 14, 15)})),
             listed(("max own 1", 0), ("split q", 2), ("split k", 2), ("max own 0", 1)),
             listed(("load x", 3), ("max own 1", 0), ("store g", 1), ("max own 0", 1), ("stack q", 2), ("stack k", 2))),
        Slot(("own", n(1)), ("own", n(2)),
             numbered((0, {1: "ctx own 1", 3: "ctxT", 4: "o", 6: "rq"}), (1, {5: "max own 1", 10: "ctx own 0"}),
                      (2, {2: "ffn up 2", 7: "v", 8: "ffn y", 13: "max own 0"})),
             listed(("max own 1", 1), ("split rq", 0), ("xn", 3), ("max own 0", 2)),
             listed(("max own 1", 1), ("stack rq", 0), ("store g", 2), ("load x", 4), ("max own 0", 2)),
             stats=(0, n(3))),
        Slot(("own", n(2)), ("past", n(0)),
             numbered((0, {13: "max past 0"}), (1, {1: "ctx own 1", 3: "ctxT", 4: "o", 6: "rq"}),
                      (2, {5: "max own 1", 10: "ctx own 0"}), (3, {7: "xnT", 8: "q", 9: "k", 11: "v", **ffn(12, 14)})),
             listed(("max own 1", 2), ("split rq", 1), ("split q", 3), ("max past 0", 0), ("split k", 3)),
             listed(("max own 1", 2), ("stack rq", 1), ("stack q", 3), ("max past 0", 0), ("stack k", 3)),
             stats=(1, n(4))),
        Slot(("past", n(0)), ("past", n(1)),
             numbered((2, {1: "ctx own 1", 3: "ctxT", 4: "o", 7: "rq"}), (0, {5: "max past 1", **CTX_PAST}),
                      (3, {2: "ffn gate 1", 8: "ffn up 1", 9: "ffn gate 2"}), (1, {13: "max past 0"})),
             listed(("max past 1", 0), ("split rq", 2), ("max past 0", 1), ("xn", 4)),
             listed(("load late", 0), ("max past 1", 0), ("max past 0", 1), ("stack rq", 2))),
        Slot(("past", n(1)), ("own", n(3)),
             numbered((0, {1: "ctx past 3", 3: "rctxT", 4: "gate", 7: "fin"}), (1, {5: "max past 1", **CTX_PAST}),
                      (3, {13: "max own 0", 15: "ffn up 2"})),
             listed(("rsum", 0), ("mix", 0), ("max past 1", 1), ("gated", 0), ("max own 0", 3)),
             listed(("max past 1", 1), ("store out", 0), ("load late", 1), ("max own 0", 3))),
    ]


def last_slots():
    n = lambda i: Count(0, i)
    L = BATCH - 1
    a = odd_slot(n(L - 2))
    a.small.update(numbered((L - 1, dict(zip((11, 14, 15), ("ffn gate 0", "ffn up 0", "ffn gate 1"))))))
    a.stats = (8, n(L))
    return [
        a,
        Slot(("past", n(L - 3)), ("own", n(L - 1)),
             numbered((L - 3, {5: "max past 1", **CTX_PAST}), (L - 2, {1: "ctx own 1", 11: "ctxT", 12: "o", 15: "rq"}),
                      (L - 1, {0: "ffn up 1", 2: "ffn gate 2", 3: "ffn up 2", 13: "max own 0"}),
                      (L, {4: "xnT", 7: "q", 8: "k", 9: "v"})),
             listed(("xn", L), ("max past 1", L - 3), ("split q", L), ("split k", L), ("max own 0", L - 1)),
             listed(("load late", L - 3), ("max past 1", L - 3), ("stack q", L), ("stack k", L), ("max own 0", L - 1))),
        Slot(("own", n(L - 1)), ("own", n(L)),
             numbered((L - 3, {1: "ctx past 3", 7: "rctxT", 9: "gate", 12: "fin"}),
                      (L - 1, {5: "max own 1", 2: "ffn y", 10: "ctx own 0"}),
                      (L, {**ffn(3, 4, 6, 8, 11, 14), 13: "max own 0"})),
             listed(("split rq", L - 2), ("rsum", L - 3), ("max own 1", L - 1), ("mix", L - 3), ("gated", L - 3),
                    ("max own 0", L)),
             listed(("stack rq", L - 2), ("max own 1", L - 1), ("store g", L - 1), ("store out", L - 3), ("max own 0", L))),
        Slot(("own", n(L)), ("past", n(L - 2)),
             numbered((L - 1, {1: "ctx own 1", 3: "ctxT", 4: "o", 6: "rq"}),
                      (L, {5: "max own 1", 7: "ffn y", 10: "ctx own 0"}), (L - 2, {13: "max past 0"})),
             listed(("max own 1", L), ("split rq", L - 1), ("max past 0", L - 2)),
             listed(("max own 1", L), ("stack rq", L - 1), ("store g", L), ("load late", L - 2), ("max past 0", L - 2))),
        Slot(("past", n(L - 2)), ("past", n(L - 1)),
             numbered((L, {1: "ctx own 1", 3: "ctxT", 4: "o", 7: "rq"}), (L - 1, {13: "max past 0"}),
                      (L - 2, {5: "max past 1", **CTX_PAST})),
             listed(("max past 1", L - 2), ("split rq", L), ("max past 0", L - 1)),
             listed(("max past 1", L - 2), ("stack rq", L), ("max past 0", L - 1))),
        Slot(("past", n(L - 1)), ("past", n(L)),
             numbered((L - 2, {1: "ctx past 3", 3: "rctxT", 4: "gate", 7: "fin"}), (L, {13: "max past 0"}),
                      (L - 1, {5: "max past 1", **CTX_PAST})),
             listed(("rsum", L - 2), ("mix", L - 2), ("max past 1", L - 1), ("gated", L - 2), ("max past 0", L)),
             listed(("max past 1", L - 1), ("store out", L - 2), ("load late", L - 1), ("max past 0", L))),
        Slot(("past", n(L)), None,
             numbered((L - 1, {1: "ctx past 3", 3: "rctxT", 4: "gate", 8: "fin"}),
                      (L, {5: "max past 1", 7: "ctx past 0", 10: "ctx past 1", 14: "ctx past 2"})),
             listed(("rsum", L - 1), ("mix", L - 1), ("max past 1", L), ("gated", L - 1)),
             listed(("max past 1", L), ("store out", L - 1), ("load late", L))),
        Slot(None, None, numbered((L, {1: "ctx past 3", 3: "rctxT", 4: "gate", 5: "fin"})),
             listed(("rsum", L), ("mix", L), ("gated", L)), listed(("store out", L))),
    ]


LOOP_FIRST = 3
TURNS = (BATCH - 3 - LOOP_FIRST) // 2


def loop_slots():
    i = Count(2, LOOP_FIRST)
    return [odd_slot(i), even_slot(i), odd_slot(i + 1), even_slot(i + 1)]


def build(nc, x, past, weights, columns, rows, w_gate, w_up, w_down, out):
    with ExitStack() as ctx:
        def sb(name, shape, dt):
            return ctx.enter_context(nc.sbuf_tensor(name, shape, dt))

        def psum(name, shape, dt):
            return ctx.enter_context(nc.psum_tensor(name, shape, dt))

        def sem(name):
            return ctx.enter_context(nc.semaphore(name))

        W = sb("W", [128, 9, H], F32)
        Wq, Wk, Wv, Wo, Wrq, Wrk, Wrv, Wg_own, Wg_past = (W[:, n, :] for n in range(9))
        cols = sb("cols", [128, 6], F32)
        bq, bk, bo, brq, brk, bg = (cols[:, n:n + 1] for n in range(6))
        half_bg = sb("half_bg", [128, 1], F32)
        brows = sb("brows", [128, 2, H], F32)
        wint = sb("wint", [128, 3, HIDDEN], I32)
        wffn = sb("wffn", [128, 3, HIDDEN], F32)
        ident = sb("ident", [128, 128], F32)
        identb = sb("identb", [128, 128], BF16)
        minus_half = sb("minus_half", [128, ST], F32)
        ones_rows = sb("ones_rows", [32, 3, S], BF16)
        x_in = sb("x_in", [128, ST, H], F32)
        bn = sb("bn", [128, ST, 6], F32)
        mean_var = sb("mean_var", [128, ST, 2], F32)
        var_eps = sb("var_eps", [128, ST], F32)
        rstd = sb("rstd", [128, ST], F32)
        xn = sb("xn", [128, ST, H], F32)
        xnT = sb("xnT", [128, S], F32)
        flat = {n: sb(f"flat_{n}", [128, S], F32) for n in ("q", "k", "rq")}
        rest = sb("rest", [128, S], F32)
        parts = {n: sb(f"parts_{n}", [128, PARTS, S], BF16) for n in ("q", "k", "rq")}
        stack_q = [sb(f"stack_q{p}", [128, PAIRS, S], BF16) for p in range(2)]
        stack_k = [sb(f"stack_k{p}", [128, PAIRS, S], BF16) for p in range(2)]
        stack_rq = [sb(f"stack_rq{p}", [128, PAIRS, S], BF16) for p in range(2)]
        stack_rq.append(stack_q[BATCH % 2])
        stack_rk = sb("stack_rk", [128, PAIRS, S], BF16)
        values = [sb(f"values{p}", [128, ST, HEADS, 32], F32) for p in range(2)]
        past_values = sb("past_values", [128, ST, HEADS, 32], F32)
        MW = {"own": 1, "past": PAST}
        top = {n: sb(f"top_{n}", [128, 2, ST, 2, MW[n], PAIRS // 2], F32) for n in MW}
        top_rest = {n: sb(f"top_rest_{n}", [128, ST * 2 * MW[n], PAIRS // 2], F32) for n in MW}
        top_parts = {n: sb(f"top_parts_{n}", [128, 2, ST, 2 * MW[n], PARTS, PAIRS // 2], BF16) for n in MW}
        TR = {n: 2 * MW[n] * PARTS * (PAIRS // 2) for n in MW}
        TB = {n: 96 // TR[n] for n in MW}
        topT = {n: sb(f"topT_{n}", [96, 2, S // TB[n]], BF16) for n in MW}
        probs = sb("probs", [128, PBUF, QUAD, S], F32)
        U = sb("U", [128, 2, S], F32)
        recip = sb("recip", [128, ST, QUAD, 2], F32)
        ctx_own = sb("ctx_own", [128, ST, H], F32)
        ctx_past = sb("ctx_past", [128, PAST, ST, H], F32)
        ctx_sum = sb("ctx_sum", [128, ST, H], F32)
        ctxT = sb("ctxT", [128, S], F32)
        oT = [sb(f"oT{p}", [128, S], F32) for p in range(3)]
        rT = sb("rT", [128, S], F32)
        tanh_g = sb("tanh_g", [128, S], F32)
        diff = sb("diff", [128, S], F32)
        both = sb("both", [128, S], F32)
        mixed = sb("mixed", [128, S], F32)
        product = sb("product", [128, S], F32)
        tanh_f = sb("tanh_f", [128, S], F32)
        hg = sb("hg", [128, S], F32)
        hT = sb("hT", [128, NB, S], F32)
        g_new = sb("g_new", [128, S], F32)
        g_late = sb("g_late", [128, S], F32)
        x_late = sb("x_late", [128, ST, H], F32)
        result = sb("result", [128, ST, H], F32)

        MX = [psum(f"MX{n}", [128, S], F32) for n in range(RING)]
        SC = [psum(f"SC{n}", [128, S], F32) for n in range(RING)]
        CT = psum("CT", [128, S], F32)
        Z = psum("Z", [128, S], F32)
        Zt = Z[:, :].rearrange("p (s h) -> p s h", s=ST)
        Zb = Z[:, :].bitcast(BF16)

        parts_d = {n: nc.dram_tensor(f"parts_{n}_d", [PARTS, 128, S], BF16).ap() for n in ("q", "k", "rq")}
        top_d = {n: nc.dram_tensor(f"top_{n}_d", [2, TR[n], S], BF16).ap() for n in MW}
        g_d = nc.dram_tensor("g_d", [BATCH, 128, S], F32).ap()

        qk_weights_loaded = sem("qk_weights_loaded")
        rest_loaded = sem("rest_loaded")
        ident_steps = sem("ident_steps")
        minus_half_made = sem("minus_half_made")
        ones_rows_made = sem("ones_rows_made")
        ones_loaded = sem("ones_loaded")
        values_cleared = sem("values_cleared")
        values_ready = sem("values_ready")
        weights_ready = sem("weights_ready")
        half_bg_made = sem("half_bg_made")
        past_split = sem("past_split")
        past_stored = sem("past_stored")
        past_stacked = sem("past_stacked")
        x_loaded = sem("x_loaded")
        bn_done = sem("bn_done")
        stats_done = sem("stats_done")
        rstd_steps = sem("rstd_steps")
        xn_made = sem("xn_made")
        filled = {}
        emptied = {}
        TIMES = {"max own": 2, "max past": 2, "ctx own": 2, "ctx past": 4, "ffn gate": NB, "ffn up": NB}
        for n in ("past T", "past k", "past v", "xnT", "q", "k", "v", "max own", "max past", "ctx own", "ctx past", "ctxT", "o", "rq", "rctxT",
                  "gate", "fin", "ffn gate", "ffn up", "ffn y"):
            filled[n] = sem("filled_" + n.replace(" ", "_"))
            emptied[n] = sem("emptied_" + n.replace(" ", "_"))
        tanh_done = {n: sem("tanh_" + n.replace(" ", "_")) for n in ("ffn gate", "ffn y")}
        split_steps = {n: sem(f"split_steps_{n}") for n in ("q", "k", "rq")}
        parts_stored = {n: sem(f"parts_stored_{n}") for n in ("q", "k", "rq")}
        stacked = {n: sem(f"stacked_{n}") for n in ("q", "k", "rq")}
        max_scored = sem("max_scored")
        max_taken = sem("max_taken")
        scored = sem("scored")
        exp_done = sem("exp_done")
        beats_done = sem("beats_done")
        top_steps = {n: sem(f"top_steps_{n}") for n in MW}
        top_stored = {n: sem(f"top_stored_{n}") for n in MW}
        top_loaded = {n: sem(f"top_loaded_{n}") for n in MW}
        U_filled = {n: sem(f"U_filled_{n}") for n in MW}
        recip_done = {n: sem(f"recip_done_{n}") for n in MW}
        rsum_done = sem("rsum_done")
        mix_done = sem("mix_done")
        gated_steps = sem("gated_steps")
        g_stored = sem("g_stored")
        late_loaded = sem("late_loaded")
        out_stored = sem("out_stored")

        def order(task):
            name, _, n = task.rpartition(" ")
            return (name, int(n)) if n.isdigit() else (task, 0)

        def nth(task, i):
            name, n = order(task)
            return TIMES.get(name, 1) * i + (n + 1)

        def hold(engine, turn):
            if turn is not None:
                engine.nop(nofuse=True)

        UROUNDS = {"own": 2, "past": 4}
        STACKED = {"q": 128, "k": 96, "rq": 128}

        def head_rows(u):
            return 64 * (u % 2)

        block = ctx.enter_context(nc.Block())

        @block.sync
        def _(sp):
            def load_x(i, t):
                if i > 0:
                    sp.wait_ge(xn_made, i.at(t))
                src = x[bass.ds(i.at(t), 1)] if t is not None else x[i.c:i.c + 1]
                sp.dma_start(x_in[:], src.rearrange("o (s p) f -> p (o s) f", p=128)).then_inc(x_loaded, 16)

            def stack_parts(dst, src, backwards, raised):
                for par in range(2):
                    v = src.rearrange("j (par d pos) s -> par j d (pos s)", par=2, pos=PAIRS)[par]
                    row = 64 * par
                    for n in (3, 2, 1):
                        take = v[PARTS - n:PARTS] if backwards else v[0:n]
                        sp.dma_start(dst[row:row + n * D].rearrange("p a b -> p (a b)"), take).then_inc(raised, 16)
                        row += n * D

            def stack_task(name, i, t, dst, kind):
                sp.wait_ge(split_steps[name], (4 * i + 4).at(t))
                if i > 0:
                    sp.wait_ge(stacked[name], (STACKED[name] * i).at(t))
                elif name == "rq":
                    sp.wait_ge(past_stacked, 96)
                sp.dma_start(parts_d[name].rearrange("j p s -> p j s"), parts[name][:]).then_inc(parts_stored[name], 16)
                sp.wait_ge(parts_stored[name], (16 * i + 16).at(t))
                if name == "rq" and rq_buffer(i) == 2:
                    sp.wait_ge(scored, (TILES * (stage("own", i - 1) + 1)).at(t))
                elif i - 1 > 0:
                    sp.wait_ge(scored, (TILES * (stage(kind, i - 2) + 1)).at(t))
                stack_parts(dst, parts_d[name], name == "k", stacked[name])
                if name != "k":
                    n = PARTS * MW[kind]
                    for row in (MAXROW, 64 + MAXROW):
                        sp.dma_start(dst[row:row + n], ones_rows[PARTS:PARTS + n, 0:1, :].to_broadcast([n, PAIRS, S])
                                     ).then_inc(stacked[name], 16)

            def top_task(kind, half, i, t):
                sp.wait_ge(emptied[f"max {kind}"], (2 * i + (half + 1)).at(t))
                if i > 0:
                    sp.wait_ge(top_loaded[kind], (64 * i).at(t))
                tb, r = TB[kind], TR[kind]
                for m in range(tb):
                    sp.dma_start(top_d[kind][half].rearrange("r (c m q) -> m r c q", m=tb, q=128)[m],
                                 topT[kind][m * r:(m + 1) * r, half, :].rearrange("r (c q) -> r c q", q=128)
                                 ).then_inc(top_stored[kind], 16)
                sp.wait_ge(top_stored[kind], (32 * tb * i + 16 * tb * (half + 1)).at(t))
                dst = stack_q[i.c % 2] if kind == "own" else stack_rq[rq_buffer(i)]
                n = MW[kind] * PARTS
                for par in range(2):
                    row = 64 * par + MAXROW
                    sp.dma_start(dst[row:row + n, half * 4:half * 4 + 4, :].rearrange("p a b -> p (a b)"),
                                 top_d[kind][half].rearrange("(par j pos) s -> par j (pos s)", par=2, j=n)[par]
                                 ).then_inc(top_loaded[kind], 16)

            def task(name, i, t):
                p = i.c % 2
                if name == "load x":
                    load_x(i, t)
                elif name == "stack q":
                    stack_task("q", i, t, stack_q[p], "own")
                elif name == "stack k":
                    stack_task("k", i, t, stack_k[p], "own")
                elif name == "stack rq":
                    stack_task("rq", i, t, stack_rq[rq_buffer(i)], "past")
                elif name == "stack past":
                    sp.wait_ge(past_split, 4)
                    sp.dma_start(parts_d["rq"].rearrange("j p s -> p j s"), parts["rq"][:]).then_inc(past_stored, 16)
                    sp.wait_ge(past_stored, 16)
                    stack_parts(stack_rk, parts_d["rq"], True, past_stacked)
                elif name.startswith("max"):
                    _, kind, half = name.split()
                    top_task(kind, int(half), i, t)
                elif name == "store g":
                    sp.wait_ge(emptied["ffn y"], (i + 1).at(t))
                    dst = g_d[bass.ds(i.at(t), 1)] if t is not None else g_d[i.c:i.c + 1]
                    sp.dma_start(dst.rearrange("o p s -> p (o s)"), g_new[:]).then_inc(g_stored, 16)
                elif name == "load late":
                    if i.a == 0 and i.c == 0:
                        sp.wait_ge(filled["past T"], 1)
                    sp.wait_ge(g_stored, (16 * i + 16).at(t))
                    if i > 0:
                        sp.wait_ge(out_stored, (16 * i).at(t))
                    src = g_d[bass.ds(i.at(t), 1)] if t is not None else g_d[i.c:i.c + 1]
                    sp.dma_start(g_late[:], src.rearrange("o p s -> p (o s)")).then_inc(late_loaded, 16)
                    src = x[bass.ds(i.at(t), 1)] if t is not None else x[i.c:i.c + 1]
                    sp.dma_start(x_late[:], src.rearrange("o (s p) f -> p (o s) f", p=128)).then_inc(late_loaded, 16)
                elif name == "store out":
                    sp.wait_ge(emptied["fin"], (i + 1).at(t))
                    dst = out[bass.ds(i.at(t), 1)] if t is not None else out[i.c:i.c + 1]
                    sp.dma_start(dst.rearrange("o (s p) f -> p (o s) f", p=128), result[:]).then_inc(out_stored, 16)

            sp.dma_start(x_in[:], x[0].rearrange("(s p) f -> p s f", p=128)).then_inc(x_loaded, 16)
            sp.dma_start(W[:, 0:2, :], weights[:, 0:2, :]).then_inc(qk_weights_loaded, 16)
            sp.dma_start(cols[:], columns).then_inc(qk_weights_loaded, 16)
            sp.dma_start(W[:, 2:, :], weights[:, 2:, :]).then_inc(rest_loaded, 16)
            sp.dma_start(brows[:], rows).then_inc(rest_loaded, 16)
            sp.dma_start(wint[:, 0, :], w_gate).then_inc(rest_loaded, 16)
            sp.dma_start(wint[:, 1, :], w_up).then_inc(rest_loaded, 16)
            sp.dma_start(wint[:, 2, :], w_down).then_inc(rest_loaded, 16)
            sp.dma_start(x_late[:], past.rearrange("(s p) f -> p s f", p=128)).then_inc(rest_loaded, 16)
            sp.wait_ge(ones_rows_made, 4)
            for par in range(2):
                for stack, row, n, part in (
                        (stack_k[0], 0, 2, slice(0, STACK - MAXROW)), (stack_k[1], 0, 2, slice(0, STACK - MAXROW)),
                        (stack_rk, 0, 0, slice(0, PARTS)), (stack_rk, PARTS, 1, slice(0, STACK - MAXROW - PARTS)),
                        *((q, 0, 0, slice(PARTS, PARTS + STACK - MAXROW)) for q in (*stack_q, *stack_rq[:2]))):
                    row += 64 * par + MAXROW
                    sp.dma_start(stack[row:row + part.stop - part.start],
                                 ones_rows[part, n:n + 1, :].to_broadcast([part.stop - part.start, PAIRS, S])
                                 ).then_inc(ones_loaded, 16)

            for slot in first_slots():
                for name, i in slot.sync:
                    task(name, i, None)
            with sp.Fori(0, TURNS) as turn:
                for slot in loop_slots():
                    for name, i in slot.sync:
                        task(name, i, turn)
            for slot in last_slots():
                for name, i in slot.sync:
                    task(name, i, None)
            sp.wait_ge(out_stored, 16 * BATCH)
            sp.wait_ge(g_stored, 16 * BATCH)

        @block.tensor
        def _(pe):
            def free_Z(before, t):
                if before:
                    name, i = before
                    pe.wait_ge(emptied[order(name)[0]], nth(name, i).at(t))

            def transposes(dst, src):
                for st in range(ST):
                    last = nc.tensor.transpose(dst[:, st * 128:(st + 1) * 128], src[:, st, :], ident[:])
                return last

            def small_task(name, i, before, t):
                kind, n = order(name)
                done = filled[kind]
                first = i.a == 0 and i.c == 0
                if kind == "past k" or kind == "past v":
                    pe.wait_ge(emptied["past T"], 1)
                elif kind == "q" and first:
                    pe.wait_ge(qk_weights_loaded, 32)
                elif kind == "v" and first:
                    pe.wait_ge(rest_loaded, 96)
                elif kind == "ffn gate" and first:
                    pe.wait_ge(weights_ready, 4)
                elif kind == "xnT" and first:
                    pe.wait_ge(ident_steps, 2)
                if kind == "xnT":
                    pe.wait_ge(xn_made, (i + 1).at(t))
                elif kind in ("q", "k", "v"):
                    pe.wait_ge(emptied["xnT"], (i + 1).at(t))
                elif kind in ("max own", "max past"):
                    pe.wait_ge(top_steps[kind[4:]], (8 * i + 4 * (n + 1)).at(t))
                elif kind in ("ctx own", "ctx past"):
                    pe.wait_ge(U_filled[kind[4:]], nth(name, i).at(t))
                elif kind == "ctxT":
                    pe.wait_ge(emptied["ctx own"], (2 * i + 2).at(t))
                elif kind == "o":
                    pe.wait_ge(emptied["ctxT"], (i + 1).at(t))
                elif kind == "rq":
                    pe.wait_ge(emptied["o"], (i + 1).at(t))
                elif kind == "rctxT":
                    pe.wait_ge(rsum_done, (i + 1).at(t))
                elif kind == "gate":
                    pe.wait_ge(emptied["rctxT"], (i + 1).at(t))
                elif kind == "fin":
                    pe.wait_ge(gated_steps, (3 * i + 3).at(t))
                elif kind == "ffn gate":
                    pe.wait_ge(emptied["xnT"], (i + 1).at(t))
                elif kind == "ffn up":
                    pe.wait_ge(emptied["ffn gate"], nth("ffn gate %d" % n, i).at(t))
                elif kind == "ffn y":
                    pe.wait_ge(emptied["ffn up"], (NB * i + NB).at(t))
                free_Z(before, t)
                if kind == "past T":
                    last = transposes(Z, x_late)
                elif kind == "past k":
                    last = nc.tensor.matmul(Z[:], Wrk, rT[:], start=True, stop=True)
                elif kind == "past v":
                    for st in range(ST):
                        last = nc.tensor.matmul(Z[:, st * H:(st + 1) * H], rT[:, st * 128:(st + 1) * 128], Wrv,
                                                start=True, stop=True)
                elif kind == "xnT":
                    last = transposes(Z, xn)
                elif kind == "q":
                    last = nc.tensor.matmul(Z[:], Wq, xnT[:], start=True, stop=True)
                elif kind == "k":
                    last = nc.tensor.matmul(Z[:], Wk, xnT[:], start=True, stop=True)
                elif kind == "v":
                    for st in range(ST):
                        last = nc.tensor.matmul(Z[:, st * H:(st + 1) * H], xnT[:, st * 128:(st + 1) * 128], Wv,
                                                start=True, stop=True)
                elif kind in ("max own", "max past"):
                    tb = TB[kind[4:]]
                    for c in range(ST // tb):
                        last = nc.tensor.transpose(
                            Zb[0:96, c * 128:(c + 1) * 128],
                            top_parts[kind[4:]][:, n, c * tb:(c + 1) * tb].rearrange("p s m j c -> p (s m j c)"), identb[:])
                elif kind in ("ctx own", "ctx past"):
                    src = U[:, n % 2, :].rearrange("p (s q) -> p s q", s=ST)
                    last = transposes(Z, src)
                elif kind == "ctxT":
                    last = transposes(Z, ctx_own)
                elif kind == "o":
                    last = nc.tensor.matmul(Z[:], Wo, ctxT[:], start=True, stop=True)
                elif kind == "rq":
                    last = nc.tensor.matmul(Z[:], Wrq, oT[o_buffer(i)][:], start=True, stop=True)
                elif kind == "rctxT":
                    last = transposes(Z, ctx_sum)
                elif kind == "gate":
                    nc.tensor.matmul(Z[:], Wg_own, oT[o_buffer(i)][:], start=True, stop=False)
                    last = nc.tensor.matmul(Z[:], Wg_past, rT[:], start=False, stop=True)
                elif kind == "fin":
                    last = transposes(Z, product[:].rearrange("p (s q) -> p s q", s=ST))
                elif kind == "ffn gate":
                    last = nc.tensor.matmul(Z[:], wffn[:, 0, n * 128:(n + 1) * 128], xnT[:], start=True, stop=True)
                elif kind == "ffn up":
                    last = nc.tensor.matmul(Z[:], wffn[:, 1, n * 128:(n + 1) * 128], xnT[:], start=True, stop=True)
                elif kind == "ffn y":
                    for b in range(NB):
                        last = nc.tensor.matmul(Z[:], wffn[:, 2, b * 128:(b + 1) * 128], hT[:, b, :],
                                                start=(b == 0), stop=(b == NB - 1))
                last.then_inc(done, 1)

            def maxima_tile(kind, i, s, beat, u, t):
                group, st = divmod(beat, ST)
                pos, row = 2 * group + u // 2, head_rows(u)
                n = 4 * beat + u
                qs, ks = (stack_q[i.c % 2], stack_k[i.c % 2]) if kind == "own" else (stack_rq[rq_buffer(i)], stack_rk)
                if n == 0:
                    if kind == "own" and i.a == 0 and i.c == 0:
                        pe.wait_ge(ones_loaded, 256)
                    if kind == "own":
                        pe.wait_ge(stacked["q"], (STACKED["q"] * (i + 1)).at(t))
                        pe.wait_ge(stacked["k"], (STACKED["k"] * (i + 1)).at(t))
                    else:
                        pe.wait_ge(stacked["rq"], (STACKED["rq"] * (i + 1)).at(t))
                        if i.a == 0 and i.c == 0:
                            pe.wait_ge(past_stacked, 96)
                if in_ring(s, n) > 0:
                    pe.wait_ge(max_taken, in_ring(s, n).at(t))
                nc.tensor.matmul(MX[n % RING][:], qs[row:row + STACK, pos, st * 128:(st + 1) * 128],
                                 ks[row:row + STACK, pos, :], start=True, stop=True).then_inc(max_scored, 1)

            def score_tile(kind, i, s, beat, u, t):
                group, st = divmod(beat, ST)
                pos, row = 2 * group + u // 2, head_rows(u)
                n = 4 * beat + u
                qs, ks = (stack_q[i.c % 2], stack_k[i.c % 2]) if kind == "own" else (stack_rq[rq_buffer(i)], stack_rk)
                if n == 0:
                    pe.wait_ge(top_loaded[kind], (64 * i + 32).at(t))
                if n == TILES // 2:
                    pe.wait_ge(top_loaded[kind], (64 * i + 64).at(t))
                if in_ring(s, n) > 0:
                    pe.wait_ge(exp_done, in_ring(s, n).at(t))
                nc.tensor.matmul(SC[n % RING][:], ks[row:row + STACK, pos, st * 128:(st + 1) * 128],
                                 qs[row:row + STACK, pos, :], start=True, stop=True).then_inc(scored, 1)

            def weigh_values(kind, i, s, beat, U_before, t):
                group, st = divmod(beat, ST)
                vals = values[i.c % 2] if kind == "own" else past_values
                per = ST * GROUPS // UROUNDS[kind]
                pe.wait_ge(exp_done, (TILES * s + 4 * (beat + 1)).at(t))
                if beat == 0 and kind == "own":
                    pe.wait_ge(emptied["v"], (i + 1).at(t))
                if beat == 0 and kind == "past" and i.a == 0 and i.c == 0:
                    pe.wait_ge(emptied["past v"], 1)
                if beat % per == 0 and U_before:
                    k0, v0 = U_before
                    pe.wait_ge(U_filled[k0], v0.at(t))
                for u in range(QUAD):
                    last = nc.tensor.matmul(CT[32 * u:32 * u + 32, :], vals[:, st, FIRST_HEAD[group] + u, :],
                                            probs[:, beat % PBUF, u, :], start=(beat % per == 0),
                                            stop=(beat % per == per - 1), skip_group_check=True)
                last.then_inc(beats_done, 1)

            def run(slots, before, pending, U_before, t):
                for slot in slots:
                    E = slot.probs
                    for b in range(BEATS):
                        M = slot.maxima_of(b)
                        if M:
                            for u in (0, 1):
                                maxima_tile(*M[0], stage(*M[0]), M[1], u, t)
                        if E:
                            for u in (0, 1):
                                score_tile(*E, stage(*E), b, u, t)
                        if pending:
                            kind, i, beat = pending
                            s = stage(kind, i)
                            weigh_values(kind, i, s, beat, U_before, t)
                            per = BEATS // UROUNDS[kind]
                            if beat % per == per - 1:
                                U_before = (kind, UROUNDS[kind] * i + (beat // per + 1))
                        if M:
                            for u in (2, 3):
                                maxima_tile(*M[0], stage(*M[0]), M[1], u, t)
                        if E:
                            for u in (2, 3):
                                score_tile(*E, stage(*E), b, u, t)
                        if b in slot.small:
                            name, i = slot.small[b]
                            small_task(name, i, before, t)
                            before = (name, i)
                        pending = (*E, b) if E else None
                return before, pending, U_before

            before, pending, U_before = run(first_slots(), None, None, None, None)
            i = Count(2, LOOP_FIRST)
            with pe.Fori(0, TURNS) as turn:
                run(loop_slots(), (before[0], i), ("past", i - 2, BEATS - 1), ("past", 4 * (i - 2) + 3), turn)
            i = Count(0, LOOP_FIRST + 2 * TURNS)
            run(last_slots(), (before[0], i), ("past", i - 2, BEATS - 1), ("past", 4 * (i - 2) + 3), None)

        @block.scalar
        def _(act):
            def probabilities(kind, i, s, beat, u, t):
                n = 4 * beat + u
                act.wait_ge(scored, (TILES * s + (n + 1)).at(t))
                if u == 0 and BEATS * s + (beat - PBUF + 1) > 0:
                    act.wait_ge(beats_done, (BEATS * s + (beat - PBUF + 1)).at(t))
                nc.scalar.activation(probs[:, beat % PBUF, u, :], SC[n % RING][:], ACT.Exp,
                                     scale=SCALE).then_inc(exp_done, 1)

            def take_contexts(kind, i, s, beat, t):
                n = beat // (BEATS // UROUNDS[kind])
                act.wait_ge(beats_done, (BEATS * s + (beat + 1)).at(t))
                nc.scalar.activation(U[:, n % 2, :], CT[:], ACT.Copy).then_inc(U_filled[kind], 1)

            def small_task(name, i, t):
                kind, n = order(name)
                p = i.c % 2
                if kind in ("v", "past v", "ctx own", "ctx past", "fin", "ffn up"):
                    return
                act.wait_ge(filled[kind], nth(name, i).at(t))
                if kind == "past T":
                    nc.scalar.activation(rT[:], Z[:], ACT.Copy).then_inc(emptied[kind], 1)
                elif kind == "past k":
                    nc.scalar.activation(flat["rq"][:], Z[:], ACT.Identity, bias=brk).then_inc(emptied[kind], 1)
                elif kind == "xnT":
                    nc.scalar.activation(xnT[:], Z[:], ACT.Copy).then_inc(emptied[kind], 1)
                elif kind in ("q", "k", "rq"):
                    if i > 0:
                        act.wait_ge(split_steps[kind], (4 * i).at(t))
                    elif kind == "rq":
                        act.wait_ge(past_split, 4)
                    nc.scalar.activation(flat[kind][:], Z[:], ACT.Identity,
                                         bias={"q": bq, "k": bk, "rq": brq}[kind]).then_inc(emptied[kind], 1)
                elif kind in ("max own", "max past"):
                    nc.scalar.activation(topT[kind[4:]][:, n, :], Zb[0:96, 0:S // TB[kind[4:]]],
                                         ACT.Copy).then_inc(emptied[kind], 1)
                elif kind == "ctxT":
                    nc.scalar.activation(ctxT[:], Z[:], ACT.Copy).then_inc(emptied[kind], 1)
                elif kind == "o":
                    nc.scalar.activation(oT[o_buffer(i)][:], Z[:], ACT.Identity, bias=bo).then_inc(emptied[kind], 1)
                elif kind == "rctxT":
                    nc.scalar.activation(rT[:], Z[:], ACT.Copy, scale=1.0 / PAST).then_inc(emptied[kind], 1)
                elif kind == "gate":
                    nc.scalar.activation(tanh_g[:], Z[:], ACT.Tanh, bias=half_bg[:], scale=0.5).then_inc(emptied[kind], 1)
                elif kind in ("ffn gate", "ffn y"):
                    nc.scalar.activation(tanh_f[:], Z[:], ACT.Tanh, scale=0.5).then_inc(tanh_done[kind], 1)

            def run(slots, pending, t):
                for slot in slots:
                    E = slot.probs
                    for b in range(BEATS):
                        if E:
                            for u in (0, 1):
                                probabilities(*E, stage(*E), b, u, t)
                        if pending:
                            kind, i, beat = pending
                            per = BEATS // UROUNDS[kind]
                            if beat % per == per - 1:
                                take_contexts(kind, i, stage(kind, i), beat, t)
                        if E:
                            for u in (2, 3):
                                probabilities(*E, stage(*E), b, u, t)
                        if b in slot.small:
                            small_task(*slot.small[b], t)
                        pending = (*E, b) if E else None

            act.wait_ge(qk_weights_loaded, 32)
            nc.scalar.activation(half_bg[:], bg, ACT.Copy, scale=0.5).then_inc(half_bg_made, 1)
            act.wait_ge(half_bg_made, 1)

            run(first_slots(), None, None)
            i = Count(2, LOOP_FIRST)
            with act.Fori(0, TURNS) as turn:
                run(loop_slots(), ("past", i - 2, BEATS - 1), turn)
            run(last_slots(), ("past", Count(0, LOOP_FIRST + 2 * TURNS - 2), BEATS - 1), None)

        @block.vector
        def _(dve):
            def take_maxima(kind, i, s, beat, u, t):
                group, st = divmod(beat, ST)
                pos, par, n = 2 * group + u // 2, u % 2, 4 * beat + u
                half, c = divmod(pos, PAIRS // 2)
                if n % (TILES // 2) == 0 and i > 0:
                    dve.wait_ge(top_steps[kind], (8 * i - (4 if n == 0 else 0)).at(t))
                dve.wait_ge(max_scored, (TILES * s + (n + 1)).at(t))
                nc.vector.tensor_reduce(top[kind][:, half, st, par, :, c],
                                        MX[n % RING][:].rearrange("p (w k) -> p w k", w=MW[kind]),
                                        AX_X, ALU.max, negate=True).then_inc(max_taken, 1)

            def small_task(name, i, t):
                kind, n = order(name)
                if kind == "past v":
                    dve.wait_ge(filled[kind], 1)
                    dve.wait_ge(values_ready, 6)
                    for a in range(2):
                        last = nc.vector.tensor_tensor(
                            past_values[:, 2 * a:2 * a + 2, :, SLOT * a:SLOT * a + D],
                            Zt[:, 2 * a:2 * a + 2, :].rearrange("p s (h d) -> p s h d", d=D),
                            brows[:, 1:2, :].rearrange("p o (h d) -> p o h d", d=D).to_broadcast([128, 2, HEADS, D]),
                            ALU.add)
                    last.then_inc(emptied[kind], 1)
                elif kind == "v":
                    dve.wait_ge(filled[kind], (i + 1).at(t))
                    if i.a == 0 and i.c == 0:
                        dve.wait_ge(values_ready, 6)
                    if i - 1 > 0:
                        dve.wait_ge(beats_done, (BEATS * (stage("own", i - 2) + 1)).at(t))
                    for a in range(2):
                        last = nc.vector.tensor_tensor(
                            values[i.c % 2][:, :, 8 * a:8 * a + 8, SLOT * a:SLOT * a + D],
                            Zt[:, :, 64 * a:64 * a + 64].rearrange("p s (h d) -> p s h d", d=D),
                            brows[:, 0:1, 64 * a:64 * a + 64].rearrange("p o (h d) -> p o h d", d=D).to_broadcast([128, ST, 8, D]),
                            ALU.add)
                    last.then_inc(emptied[kind], 1)
                elif kind in ("ctx own", "ctx past"):
                    k2 = kind[4:]
                    dve.wait_ge(filled[kind], nth(name, i).at(t))
                    if k2 == "past" and n == 0 and i > 0:
                        dve.wait_ge(rsum_done, i.at(t))
                    zc = Z[:].rearrange("p (s q c) -> p s q c", s=ST, q=QUAD)
                    nc.vector.reciprocal(recip[:], zc[:, :, :, D:D + SLOT + 1:SLOT]).then_inc(recip_done[k2], 1)
                    dve.wait_ge(recip_done[k2], nth(name, i).at(t))
                    for a in range(2):
                        if k2 == "own":
                            c0 = (FIRST_HEAD[2 * n + a]) * D
                            dst = ctx_own[:, :, c0:c0 + QUAD * D]
                        else:
                            c0 = FIRST_HEAD[n] * D
                            dst = ctx_past[:, a, :, c0:c0 + QUAD * D]
                        last = nc.vector.tensor_tensor(dst.rearrange("p s (q d) -> p s q d", d=D),
                                                       zc[:, :, :, SLOT * a:SLOT * a + D],
                                                       recip[:, :, :, a:a + 1].to_broadcast([128, ST, QUAD, D]), ALU.mult)
                    last.then_inc(emptied[kind], 1)
                elif kind == "fin":
                    dve.wait_ge(filled[kind], (i + 1).at(t))
                    dve.wait_ge(late_loaded, (32 * i + 32).at(t))
                    nc.vector.scalar_tensor_tensor(out=result[:], in0=Zt, scalar=0.25, in1=x_late[:],
                                                   op0=ALU.mult, op1=ALU.add).then_inc(emptied[kind], 1)
                elif kind == "ffn gate":
                    dve.wait_ge(tanh_done[kind], nth(name, i).at(t))
                    nc.vector.scalar_tensor_tensor(out=hg[:], in0=tanh_f[:], scalar=1.0, in1=Z[:],
                                                   op0=ALU.add, op1=ALU.mult).then_inc(emptied[kind], 1)
                elif kind == "ffn up":
                    dve.wait_ge(filled[kind], nth(name, i).at(t))
                    nc.vector.tensor_tensor(hT[:, n, :], hg[:], Z[:], ALU.mult).then_inc(emptied[kind], 1)
                elif kind == "ffn y":
                    dve.wait_ge(tanh_done[kind], (i + 1).at(t))
                    if i > 0:
                        dve.wait_ge(g_stored, (16 * i).at(t))
                    nc.vector.scalar_tensor_tensor(out=g_new[:], in0=tanh_f[:], scalar=1.0, in1=Z[:],
                                                   op0=ALU.add, op1=ALU.mult).then_inc(emptied[kind], 1)

            def statistics(i, t):
                dve.wait_ge(x_loaded, (16 * i + 16).at(t))
                for st in range(ST):
                    last = nc.vector.bn_stats(bn[:, st, :], x_in[:, st, :])
                last.then_inc(bn_done, 1)
                dve.wait_ge(bn_done, (i + 1).at(t))
                if i > 0:
                    dve.wait_ge(xn_made, i.at(t))
                hold(dve, t)
                for st in range(ST):
                    last = nc.vector.bn_aggr(mean_var[:, st, :], bn[:, st, :])
                last.then_inc(stats_done, 1)

            def run(slots, late, t):
                for slot in slots:
                    for b in range(BEATS):
                        M = slot.maxima_of(b)
                        if M:
                            for u in (0, 1):
                                take_maxima(*M[0], stage(*M[0]), M[1], u, t)
                        if slot.stats and slot.stats[0] == b:
                            statistics(slot.stats[1], t)
                        if late:
                            small_task(*late, t)
                        if M:
                            for u in (2, 3):
                                take_maxima(*M[0], stage(*M[0]), M[1], u, t)
                        late = slot.small.get(b)
                return late

            half_keys = S // PAST
            nc.vector.memset(ones_rows[:], 0.0).then_inc(ones_rows_made, 1)
            dve.wait_ge(ones_rows_made, 1)
            nc.vector.memset(ones_rows[0:PARTS, 0, 0:half_keys], 1.0).then_inc(ones_rows_made, 1)
            nc.vector.memset(ones_rows[0:PARTS, 1, half_keys:S], 1.0).then_inc(ones_rows_made, 1)
            nc.vector.memset(ones_rows[0:PARTS, 2, :], 1.0).then_inc(ones_rows_made, 1)
            statistics(Count(0, 0), None)
            dve.wait_ge(rstd_steps, 2)
            for st in range(ST):
                last = nc.vector.tensor_scalar(xn[:, st, :], x_in[:, st, :], mean_var[:, st, 0:1],
                                               rstd[:, st:st + 1], ALU.subtract, ALU.mult)
            last.then_inc(xn_made, 1)
            dve.wait_ge(rest_loaded, 96)
            for n in range(2):
                nc.vector.tensor_scalar(wffn[:, n, :], wint[:, n, :], DEQUANT, None, ALU.mult).then_inc(weights_ready, 1)
            nc.vector.tensor_scalar(wffn[:, 2, :], wint[:, 2, :], DEQUANT, 0.5, ALU.mult, ALU.mult).then_inc(weights_ready, 1)
            dve.wait_ge(ident_steps, 2)
            nc.vector.tensor_copy(identb[:], ident[:]).then_inc(weights_ready, 1)
            for n in ("q", "k"):
                part = [parts[n][:, j, :] for j in (range(PARTS) if n == "q" else reversed(range(PARTS)))]
                dve.wait_ge(emptied[n], 1)
                if n == "k":
                    dve.wait_ge(split_steps["q"], 4)
                nc.vector.tensor_copy(part[0], flat[n][:]).then_inc(split_steps[n], 1)
                dve.wait_ge(split_steps[n], 1)
                nc.vector.tensor_tensor(rest[:], flat[n][:], part[0], ALU.subtract).then_inc(split_steps[n], 1)
                dve.wait_ge(split_steps[n], 2)
                nc.vector.tensor_copy(part[1], rest[:]).then_inc(split_steps[n], 1)
                dve.wait_ge(split_steps[n], 3)
                nc.vector.tensor_tensor(part[2], rest[:], part[1], ALU.subtract).then_inc(split_steps[n], 1)

            late = run(first_slots(), None, None)
            i = Count(2, LOOP_FIRST)
            with dve.Fori(0, TURNS) as turn:
                run(loop_slots(), (late[0], i), turn)
            run(last_slots(), (late[0], Count(0, LOOP_FIRST + 2 * TURNS)), None)

        @block.gpsimd
        def _(pool):
            def split(src, res, out_parts, raised, base, t):
                hold(pool, t)
                nc.gpsimd.tensor_copy(out_parts[0], src).then_inc(raised, 1)
                pool.wait_ge(raised, (base + 1).at(t))
                nc.gpsimd.tensor_tensor(res, src, out_parts[0], ALU.subtract).then_inc(raised, 1)
                pool.wait_ge(raised, (base + 2).at(t))
                hold(pool, t)
                nc.gpsimd.tensor_copy(out_parts[1], res).then_inc(raised, 1)
                pool.wait_ge(raised, (base + 3).at(t))
                nc.gpsimd.tensor_tensor(out_parts[2], res, out_parts[1], ALU.subtract).then_inc(raised, 1)

            def top_split(kind, half, i, t):
                s = stage(kind, i)
                src = top[kind][:, half].rearrange("p s r w c -> p (s r w) c")
                dst = top_parts[kind][:, half].rearrange("p s m j c -> p (s m) j c")
                if i > 0:
                    pool.wait_ge(filled[f"max {kind}"], (2 * i + (half - 1)).at(t))
                pool.wait_ge(max_taken, (TILES * s + TILES // 2 * (half + 1)).at(t))
                split(src, top_rest[kind][:], [dst[:, :, j, :] for j in range(PARTS)],
                      top_steps[kind], 8 * i + 4 * half, t)

            def value_operands():
                for v in (values[0], values[1], past_values):
                    nc.gpsimd.memset(v[:], 0.0).then_inc(values_cleared, 1)
                pool.wait_ge(values_cleared, 3)
                for a in range(2):
                    for v in (values[0], values[1]):
                        nc.gpsimd.memset(v[:, :, 8 * a:8 * a + 8, SLOT * a + D:SLOT * a + D + 1], 1.0).then_inc(values_ready, 1)
                    nc.gpsimd.memset(past_values[:, 2 * a:2 * a + 2, :, SLOT * a + D:SLOT * a + D + 1], 1.0).then_inc(values_ready, 1)

            def task(name, i, t):
                if name.startswith("max"):
                    _, kind, half = name.split()
                    top_split(kind, int(half), i, t)
                elif name == "split past":
                    pool.wait_ge(emptied["past k"], 1)
                    pool.wait_ge(split_steps["k"], 4)
                    split(flat["rq"][:], rest[:], [parts["rq"][:, j, :] for j in reversed(range(PARTS))],
                          past_split, Count(0, 0), None)
                elif name.startswith("split"):
                    n = name.split()[1]
                    if i > 0:
                        pool.wait_ge(parts_stored[n], (16 * i).at(t))
                    elif n == "rq":
                        pool.wait_ge(past_stored, 16)
                    pool.wait_ge(emptied[n], (i + 1).at(t))
                    split(flat[n][:], rest[:], [parts[n][:, j, :] for j in
                                                (range(PARTS) if n != "k" else reversed(range(PARTS)))],
                          split_steps[n], 4 * i, t)
                elif name == "xn":
                    pool.wait_ge(stats_done, (i + 1).at(t))
                    hold(pool, t)
                    nc.gpsimd.tensor_scalar(var_eps[:], mean_var[:, :, 1], EPS, None, ALU.add).then_inc(rstd_steps, 1)
                    pool.wait_ge(rstd_steps, (2 * i + 1).at(t))
                    nc.gpsimd.tensor_tensor(rstd[:], var_eps[:], minus_half[:], ALU.pow).then_inc(rstd_steps, 1)
                    if i.a == 0 and i.c == 0:
                        value_operands()
                        return
                    if i > 0:
                        pool.wait_ge(filled["xnT"], i.at(t))
                    pool.wait_ge(rstd_steps, (2 * i + 2).at(t))
                    hold(pool, t)
                    for st in range(ST):
                        last = nc.gpsimd.tensor_scalar(xn[:, st, :], x_in[:, st, :], mean_var[:, st, 0:1],
                                                       rstd[:, st:st + 1], ALU.subtract, ALU.mult)
                    last.then_inc(xn_made, 1)
                elif name == "rsum":
                    pool.wait_ge(emptied["ctx past"], (4 * i + 4).at(t))
                    nc.gpsimd.tensor_tensor(ctx_sum[:], ctx_past[:, 0], ctx_past[:, 1], ALU.add).then_inc(rsum_done, 1)
                elif name == "mix":
                    pool.wait_ge(emptied["rctxT"], (i + 1).at(t))
                    nc.gpsimd.tensor_tensor(diff[:], rT[:], oT[o_buffer(i)][:], ALU.subtract).then_inc(mix_done, 1)
                    nc.gpsimd.tensor_tensor(both[:], rT[:], oT[o_buffer(i)][:], ALU.add).then_inc(mix_done, 1)
                elif name == "gated":
                    pool.wait_ge(mix_done, (2 * i + 2).at(t))
                    pool.wait_ge(emptied["gate"], (i + 1).at(t))
                    nc.gpsimd.tensor_tensor(mixed[:], tanh_g[:], diff[:], ALU.mult).then_inc(gated_steps, 1)
                    pool.wait_ge(gated_steps, (3 * i + 1).at(t))
                    nc.gpsimd.tensor_tensor(mixed[:], mixed[:], both[:], ALU.add).then_inc(gated_steps, 1)
                    pool.wait_ge(late_loaded, (32 * i + 32).at(t))
                    pool.wait_ge(gated_steps, (3 * i + 2).at(t))
                    nc.gpsimd.tensor_tensor(product[:], mixed[:], g_late[:], ALU.mult).then_inc(gated_steps, 1)

            nc.gpsimd.memset(ident[:], 0.0).then_inc(ident_steps, 1)
            nc.gpsimd.memset(minus_half[:], -0.5).then_inc(minus_half_made, 1)
            pool.wait_ge(ident_steps, 1)
            nc.gpsimd.affine_select(out=ident[:], in_=ident[:], compare_op=ALU.not_equal, fill=1.0, base=0,
                                    pattern=[[-1, 128]], channel_multiplier=1).then_inc(ident_steps, 1)
            pool.wait_ge(minus_half_made, 1)

            for slot in first_slots():
                for name, i in slot.pool:
                    task(name, i, None)
            with pool.Fori(0, TURNS) as turn:
                for slot in loop_slots():
                    for name, i in slot.pool:
                        task(name, i, turn)
            for slot in last_slots():
                for name, i in slot.pool:
                    task(name, i, None)
    return nc


def kernel(**inputs):
    import numpy as np
    import concourse.bacc as bacc
    from concourse.bass_utils import run_bass_kernel_spmd

    a = {n.removeprefix("L0_"): np.asarray(v) for n, v in inputs.items()}
    order = []
    for par in range(2):
        for d in range(D):
            for pos in range(PAIRS):
                head = FIRST_HEAD[pos // 2] + 2 * (pos % 2) + par
                order.append(head * D + d)
    order = np.array(order)
    gate = a["attn_Wg"]
    weights = np.stack([a["attn_Wq"][:, order], a["attn_Wk"][:, order], a["attn_Wv"], a["attn_Wo"],
                        a["attn_Wrq"][:, order], a["attn_Wrk"][:, order], a["attn_Wrv"], gate[:H], gate[H:]], axis=1)
    columns = np.stack([a["attn_bq"][order], a["attn_bk"][order], a["attn_bo"], a["attn_brq"][order],
                        a["attn_brk"][order], a["attn_bg"]], axis=1)
    rows = np.broadcast_to(np.stack([a["attn_bv"], a["attn_brv"]])[None], (128, 2, H))
    down = a["ffn_w_down"].T.reshape(NB, 128, H).transpose(1, 0, 2).reshape(128, NB * H)
    arrays = {
        "x": a["attn_hidden_states"], "past": a["attn_past_states"].reshape(S, H), "weights": weights,
        "columns": columns, "rows": rows, "w_gate": a["ffn_w_gate"].T, "w_up": a["ffn_w_up"].T, "w_down": down,
    }
    arrays = {n: np.ascontiguousarray(v) for n, v in arrays.items()}
    nc = bacc.Bacc("TRN2", target_bir_lowering=False, num_devices=1)
    nc.disable_value_cache = True
    args = [nc.dram_tensor(n, v.shape, mybir.dt.from_np(v.dtype), kind="ExternalInput").ap() for n, v in arrays.items()]
    out = nc.dram_tensor("out", (BATCH, S, H), F32, kind="ExternalOutput").ap()
    build(nc, *args, out)
    r = run_bass_kernel_spmd(nc, [arrays], core_ids=[0])
    return r.results[0]["out"]
```

```python
from contextlib import ExitStack

import concourse.bass as bass
from concourse import mybir

F32 = mybir.dt.float32
BF16 = mybir.dt.bfloat16
I32 = mybir.dt.int32
ALU = mybir.AluOpType
ACT = mybir.ActivationFunctionType
AX_X = mybir.AxisListType.X

BATCH = 16
S = 512
H = 128
HEADS = 16
D = H // HEADS
PAST = 2
HIDDEN = 384
NB = HIDDEN // 128
ST = S // 128
SCALE = 1.0 / float(D) ** 0.5
DEQUANT = 0.007874015718698502
EPS = 1e-5

PARTS = 3
ROWS = 6 * D
MAXROW = ROWS
STACK = 64
QUAD = 4
MAXIMA_ORDER = (1, 3, 0, 2)
SCORES_ORDER = (0, 2, 1, 3)
GROUPS = HEADS // QUAD
FIRST_HEAD = [0, 8, 4, 12]
PAIRS = HEADS // 2
BEATS = GROUPS * ST
TILES = QUAD * BEATS
RING = 3
SECOND_OLDEST = (57, 59)
LAG = 4
PBUF = 4
SLOT = D + 1



class Count:

    def __init__(self, a, c):
        self.a, self.c = a, c

    def __add__(self, n):
        return Count(self.a, self.c + n)

    def __sub__(self, n):
        return Count(self.a, self.c - n)

    def __mul__(self, n):
        return Count(self.a * n, self.c * n)

    __rmul__ = __mul__

    def __gt__(self, n):
        assert not (self.c <= n and self.a > 0), "zero in the first turn"
        return self.c > n

    def at(self, turn):
        return self.c if turn is None else turn * self.a + self.c


def stage(kind, i):
    n = i.c if i.a == 0 else None
    if kind == "own":
        return Count(0, n) if n in (0, 1, 2) else Count(0, 2 * n - 2) if n == BATCH - 1 else 2 * i - 1
    if n == 0 or n == BATCH - 3:
        return Count(0, 2 * n + 3)
    return Count(0, 2 * n + 1) if n == BATCH - 1 else 2 * i + 2


def rq_buffer(i):
    return 2 if i.a == 0 and i.c == BATCH - 1 else i.c % 2


def o_buffer(i):
    return 2 if i.a == 0 and i.c in (0, BATCH - 1) else i.c % 2


def ring():
    order, last = list(range(RING)), {b: b - RING for b in range(RING)}
    banks, before = [], []
    for n in range(TILES):
        bank = order.pop(1 if n in SECOND_OLDEST else 0)
        order.append(bank)
        banks.append(bank)
        before.append(last[bank])
        last[bank] = n
    assert TILES % RING == 1 and order == list(range(RING))
    return banks, before


BANK, BEFORE = ring()


def in_ring(s, n):
    return TILES * s + (BEFORE[n] + 1)


class Slot:

    def __init__(self, probs, maxima, small, pool, sync, stats=None):
        self.probs, self.maxima, self.small = probs, maxima, small
        self.pool, self.sync, self.stats = pool, sync, stats

    def maxima_of(self, b):
        if self.probs is None:
            return (self.maxima, b) if self.maxima and b < BEATS - LAG else None
        if b < LAG:
            return self.probs, BEATS - LAG + b
        return (self.maxima, b - LAG) if self.maxima else None


def odd_slot(i):
    small = {0: ("xnT", i + 1), 1: ("ctx past 3", i - 2), 3: ("q", i + 1), 4: ("k", i + 1),
             5: ("max own 1", i), 6: ("ffn y", i), 7: ("rctxT", i - 2), 9: ("gate", i - 2), 12: ("fin", i - 2),
             13: ("max past 0", i - 1), 14: ("v", i + 1), 15: ("ctx own 0", i)}
    pool = [("rsum", i - 2), ("max own 1", i), ("split q", i + 1), ("split k", i + 1), ("mix", i - 2),
            ("gated", i - 2), ("max past 0", i - 1)]
    sync = [("load x", i + 2), ("max own 1", i), ("store g", i), ("stack q", i + 1), ("stack k", i + 1),
            ("store out", i - 2), ("max past 0", i - 1)]
    return Slot(("own", i), ("past", i - 1), small, pool, sync)


def even_slot(i):
    small = {1: ("ffn gate 0", i + 1), 2: ("ctx own 1", i), 3: ("ctxT", i), 4: ("o", i),
             5: ("max past 1", i - 1), 6: ("ctx past 0", i - 1), 7: ("rq", i), 8: ("ffn up 0", i + 1),
             9: ("ffn gate 1", i + 1), 10: ("ctx past 1", i - 1), 11: ("ffn up 1", i + 1),
             12: ("max own 0", i + 1), 13: ("ffn gate 2", i + 1), 14: ("ctx past 2", i - 1),
             15: ("ffn up 2", i + 1)}
    pool = [("max past 1", i - 1), ("split rq", i), ("max own 0", i + 1), ("xn", i + 2)]
    sync = [("load late", i - 1), ("max past 1", i - 1), ("stack rq", i), ("max own 0", i + 1)]
    return Slot(("past", i - 1), ("own", i + 1), small, pool, sync, stats=(4, i + 2))


def numbered(*tasks):
    return {b: (name, Count(0, i)) for i, beats in tasks for b, name in beats.items()}


def listed(*tasks):
    return [(name, Count(0, i)) for name, i in tasks]


def ffn(*beats):
    return dict(zip(beats, ("ffn gate 0", "ffn up 0", "ffn gate 1", "ffn up 1", "ffn gate 2", "ffn up 2")))


CTX_PAST = {6: "ctx past 0", 10: "ctx past 1", 14: "ctx past 2"}


def first_slots():
    n = lambda i: Count(0, i)
    return [
        Slot(None, None,
             numbered((0, {0: "xnT", 1: "q", 2: "k", 3: "v", 4: "past T", 5: "past k"})),
             listed(("xn", 0), ("xn", 1), ("split past", 0)),
             listed(("load x", 1), ("store q", 0), ("store k", 0), ("stack q", 0), ("stack k", 0), ("stack constants", 0), ("stack past", 0)),
             stats=(5, n(1))),
        Slot(None, ("own", n(0)),
             numbered((0, {0: "past v", **ffn(1, 2, 3, 4, 5, 6), 9: "max own 0", 12: "ffn y"}),
                      (1, {7: "xnT", 8: "q", 10: "k", 11: "v"})),
             listed(("max own 0", 0), ("split q", 1), ("split k", 1), ("xn", 2)),
             listed(("load x", 2), ("max own 0", 0), ("stack q", 1), ("stack k", 1), ("store g", 0)), stats=(8, n(2))),
        Slot(("own", n(0)), ("own", n(1)),
             numbered((0, {5: "max own 1", 10: "ctx own 0"}),
                      (1, {**ffn(0, 1, 2, 3, 4, 6), 7: "ffn y", 13: "max own 0"}),
                      (2, {8: "xnT", 9: "q", 11: "k", **ffn(12, 14, 15)})),
             listed(("max own 1", 0), ("split q", 2), ("max own 0", 1), ("split k", 2)),
             listed(("load x", 3), ("max own 1", 0), ("store g", 1), ("max own 0", 1), ("stack q", 2), ("stack k", 2))),
        Slot(("own", n(1)), ("own", n(2)),
             numbered((0, {1: "ctx own 1", 3: "ctxT", 4: "o", 6: "rq"}), (1, {5: "max own 1", 10: "ctx own 0"}),
                      (2, {0: "ffn up 1", 2: "ffn gate 2", 7: "v", 8: "ffn up 2", 9: "ffn y", 13: "max own 0"})),
             listed(("max own 1", 1), ("split rq", 0), ("xn", 3), ("max own 0", 2)),
             listed(("max own 1", 1), ("stack rq", 0), ("store g", 2), ("load x", 4), ("max own 0", 2)),
             stats=(0, n(3))),
        Slot(("own", n(2)), ("past", n(0)),
             numbered((0, {13: "max past 0"}), (1, {1: "ctx own 1", 3: "ctxT", 4: "o", 6: "rq"}),
                      (2, {5: "max own 1", 10: "ctx own 0"}), (3, {7: "xnT", 8: "q", 9: "k", 11: "v", **ffn(12, 14)})),
             listed(("max own 1", 2), ("split rq", 1), ("split q", 3), ("max past 0", 0), ("split k", 3)),
             listed(("max own 1", 2), ("stack rq", 1), ("stack q", 3), ("max past 0", 0), ("stack k", 3)),
             stats=(1, n(4))),
        Slot(("past", n(0)), ("past", n(1)),
             numbered((2, {1: "ctx own 1", 3: "ctxT", 4: "o", 7: "rq"}), (0, {5: "max past 1", **CTX_PAST}),
                      (3, {2: "ffn gate 1", 8: "ffn up 1", 9: "ffn gate 2"}), (1, {13: "max past 0"})),
             listed(("max past 1", 0), ("split rq", 2), ("max past 0", 1), ("xn", 4)),
             listed(("load late", 0), ("max past 1", 0), ("max past 0", 1), ("stack rq", 2))),
        Slot(("past", n(1)), ("own", n(3)),
             numbered((0, {1: "ctx past 3", 3: "rctxT", 4: "gate", 7: "fin"}), (1, {5: "max past 1", **CTX_PAST}),
                      (3, {13: "max own 0", 15: "ffn up 2"})),
             listed(("rsum", 0), ("mix", 0), ("max past 1", 1), ("gated", 0), ("max own 0", 3)),
             listed(("max past 1", 1), ("store out", 0), ("load late", 1), ("max own 0", 3))),
    ]


def last_slots():
    n = lambda i: Count(0, i)
    L = BATCH - 1
    a = odd_slot(n(L - 2))
    a.small.update(numbered((L - 1, dict(zip([b for b in range(BEATS) if b not in a.small and b > 2][-3:], ("ffn gate 0", "ffn up 0", "ffn gate 1"))))))
    a.stats = (8, n(L))
    return [
        a,
        Slot(("past", n(L - 3)), ("own", n(L - 1)),
             numbered((L - 3, {5: "max past 1", **CTX_PAST}), (L - 2, {1: "ctx own 1", 11: "ctxT", 12: "o", 15: "rq"}),
                      (L - 1, {0: "ffn up 1", 2: "ffn gate 2", 3: "ffn up 2", 13: "max own 0"}),
                      (L, {4: "xnT", 7: "q", 8: "k", 9: "v"})),
             listed(("xn", L), ("max past 1", L - 3), ("split q", L), ("split k", L), ("max own 0", L - 1)),
             listed(("load late", L - 3), ("max past 1", L - 3), ("stack q", L), ("stack k", L), ("max own 0", L - 1))),
        Slot(("own", n(L - 1)), ("own", n(L)),
             numbered((L - 3, {1: "ctx past 3", 7: "rctxT", 9: "gate", 12: "fin"}),
                      (L - 1, {5: "max own 1", 2: "ffn y", 10: "ctx own 0"}),
                      (L, {**ffn(3, 4, 6, 8, 11, 14), 13: "max own 0"})),
             listed(("split rq", L - 2), ("rsum", L - 3), ("max own 1", L - 1), ("mix", L - 3), ("gated", L - 3),
                    ("max own 0", L)),
             listed(("stack rq", L - 2), ("max own 1", L - 1), ("store g", L - 1), ("store out", L - 3), ("max own 0", L))),
        Slot(("own", n(L)), ("past", n(L - 2)),
             numbered((L - 1, {1: "ctx own 1", 3: "ctxT", 4: "o", 6: "rq"}),
                      (L, {5: "max own 1", 7: "ffn y", 10: "ctx own 0"}), (L - 2, {13: "max past 0"})),
             listed(("max own 1", L), ("split rq", L - 1), ("max past 0", L - 2)),
             listed(("max own 1", L), ("stack rq", L - 1), ("store g", L), ("load late", L - 2), ("max past 0", L - 2))),
        Slot(("past", n(L - 2)), ("past", n(L - 1)),
             numbered((L, {1: "ctx own 1", 3: "ctxT", 4: "o", 7: "rq"}), (L - 1, {13: "max past 0"}),
                      (L - 2, {5: "max past 1", **CTX_PAST})),
             listed(("max past 1", L - 2), ("split rq", L), ("max past 0", L - 1)),
             listed(("max past 1", L - 2), ("stack rq", L), ("max past 0", L - 1))),
        Slot(("past", n(L - 1)), ("past", n(L)),
             numbered((L - 2, {1: "ctx past 3", 3: "rctxT", 4: "gate", 7: "fin"}), (L, {13: "max past 0"}),
                      (L - 1, {5: "max past 1", **CTX_PAST})),
             listed(("rsum", L - 2), ("mix", L - 2), ("max past 1", L - 1), ("gated", L - 2), ("max past 0", L)),
             listed(("max past 1", L - 1), ("store out", L - 2), ("load late", L - 1), ("max past 0", L))),
        Slot(("past", n(L)), None,
             numbered((L - 1, {1: "ctx past 3", 3: "rctxT", 4: "gate", 8: "fin"}),
                      (L, {5: "max past 1", 7: "ctx past 0", 10: "ctx past 1", 14: "ctx past 2"})),
             listed(("rsum", L - 1), ("mix", L - 1), ("max past 1", L), ("gated", L - 1)),
             listed(("max past 1", L), ("store out", L - 1), ("load late", L))),
        Slot(None, None, numbered((L, {1: "ctx past 3", 3: "rctxT", 4: "gate", 5: "fin"})),
             [], listed(("store out", L))),
    ]


LOOP_FIRST = 3
TURNS = (BATCH - 3 - LOOP_FIRST) // 2


def loop_slots():
    i = Count(2, LOOP_FIRST)
    return [odd_slot(i), even_slot(i), odd_slot(i + 1), even_slot(i + 1)]


def build(nc, x, past, weights, columns, rows, w_gate, w_up, w_down, out):
    with ExitStack() as ctx:
        def sb(name, shape, dt):
            return ctx.enter_context(nc.sbuf_tensor(name, shape, dt))

        def psum(name, shape, dt):
            return ctx.enter_context(nc.psum_tensor(name, shape, dt))

        def sem(name):
            return ctx.enter_context(nc.semaphore(name))

        W = sb("W", [128, 9, H], F32)
        Wq, Wk, Wv, Wo, Wrq, Wrk, Wrv, Wg_own, Wg_past = (W[:, n, :] for n in range(9))
        cols = sb("cols", [128, 6], F32)
        bq, bk, bo, brq, brk, bg = (cols[:, n:n + 1] for n in range(6))
        half_bg = sb("half_bg", [128, 1], F32)
        brows = sb("brows", [128, 2, H], F32)
        wint = sb("wint", [128, 3, HIDDEN], I32)
        wffn = sb("wffn", [128, 3, HIDDEN], F32)
        ident = sb("ident", [128, 128], F32)
        identb = sb("identb", [128, 128], BF16)
        minus_half = sb("minus_half", [128, ST], F32)
        ones_rows = sb("ones_rows", [32, 3, S], BF16)
        x_in = sb("x_in", [128, ST, H], F32)
        bn = sb("bn", [128, ST, 6], F32)
        mean_var = sb("mean_var", [128, ST, 2], F32)
        var_eps = sb("var_eps", [128, ST], F32)
        rstd = sb("rstd", [128, ST], F32)
        xn = sb("xn", [128, ST, H], F32)
        xnT = sb("xnT", [128, S], F32)
        flat = {n: sb(f"flat_{n}", [128, S], F32) for n in ("q", "k", "rq")}
        rest = sb("rest", [128, S], F32)
        parts = {n: sb(f"parts_{n}", [128, PARTS, S], BF16) for n in ("q", "k", "rq")}
        stack_q = [sb(f"stack_q{p}", [128, PAIRS, S], BF16) for p in range(2)]
        stack_k = [sb(f"stack_k{p}", [128, PAIRS, S], BF16) for p in range(2)]
        stack_rq = [sb(f"stack_rq{p}", [128, PAIRS, S], BF16) for p in range(2)]
        stack_rq.append(stack_q[BATCH % 2])
        stack_rk = sb("stack_rk", [128, PAIRS, S], BF16)
        values = [sb(f"values{p}", [128, ST, HEADS, 32], F32) for p in range(2)]
        past_values = sb("past_values", [128, ST, HEADS, 32], F32)
        MW = {"own": 1, "past": PAST}
        top = {n: sb(f"top_{n}", [128, 2, ST, 2, MW[n], PAIRS // 2], F32) for n in MW}
        top_rest = {n: sb(f"top_rest_{n}", [128, ST * 2 * MW[n], PAIRS // 2], F32) for n in MW}
        top_parts = {n: sb(f"top_parts_{n}", [128, 2, ST, 2 * MW[n], PARTS, PAIRS // 2], BF16) for n in MW}
        TR = {n: 2 * MW[n] * PARTS * (PAIRS // 2) for n in MW}
        TB = {n: 96 // TR[n] for n in MW}
        topT = {n: sb(f"topT_{n}", [96, 2, S // TB[n]], BF16) for n in MW}
        probs = sb("probs", [128, PBUF, QUAD, S], F32)
        U = sb("U", [128, 2, S], F32)
        recip = sb("recip", [128, ST, QUAD, 2], F32)
        ctx_own = sb("ctx_own", [128, ST, H], F32)
        ctx_past = sb("ctx_past", [128, PAST, ST, H], F32)
        ctx_sum = sb("ctx_sum", [128, ST, H], F32)
        ctxT = sb("ctxT", [128, S], F32)
        oT = [sb(f"oT{p}", [128, S], F32) for p in range(3)]
        rT = sb("rT", [128, S], F32)
        tanh_g = sb("tanh_g", [128, S], F32)
        diff = sb("diff", [128, S], F32)
        both = sb("both", [128, S], F32)
        mixed = sb("mixed", [128, S], F32)
        product = sb("product", [128, S], F32)
        tanh_f = sb("tanh_f", [128, S], F32)
        hg = sb("hg", [128, S], F32)
        hT = sb("hT", [128, NB, S], F32)
        g_new = sb("g_new", [128, S], F32)
        g_late = sb("g_late", [128, S], F32)
        x_late = sb("x_late", [128, ST, H], F32)
        result = sb("result", [128, ST, H], F32)

        MX = [psum(f"MX{n}", [128, S], F32) for n in range(RING)]
        SC = [psum(f"SC{n}", [128, S], F32) for n in range(RING)]
        CT = psum("CT", [128, S], F32)
        Z = psum("Z", [128, S], F32)
        Zt = Z[:, :].rearrange("p (s h) -> p s h", s=ST)
        Zb = Z[:, :].bitcast(BF16)

        parts_d = {n: nc.dram_tensor(f"parts_{n}_d", [PARTS, 128, S], BF16).ap() for n in ("q", "k", "rq")}
        top_d = {n: nc.dram_tensor(f"top_{n}_d", [2, TR[n], S], BF16).ap() for n in MW}
        g_d = nc.dram_tensor("g_d", [BATCH, 128, S], F32).ap()

        qk_weights_loaded = sem("qk_weights_loaded")
        rest_loaded = sem("rest_loaded")
        ident_steps = sem("ident_steps")
        minus_half_made = sem("minus_half_made")
        ones_rows_made = sem("ones_rows_made")
        ones_loaded = sem("ones_loaded")
        values_cleared = sem("values_cleared")
        values_ready = sem("values_ready")
        weights_ready = sem("weights_ready")
        half_bg_made = sem("half_bg_made")
        past_split = sem("past_split")
        past_stored = sem("past_stored")
        past_stacked = sem("past_stacked")
        x_loaded = sem("x_loaded")
        bn_done = sem("bn_done")
        stats_done = sem("stats_done")
        rstd_steps = sem("rstd_steps")
        xn_made = sem("xn_made")
        filled = {}
        emptied = {}
        TIMES = {"max own": 2, "max past": 2, "ctx own": 2, "ctx past": 4, "ffn gate": NB, "ffn up": NB}
        for n in ("past T", "past k", "past v", "xnT", "q", "k", "v", "max own", "max past", "ctx own", "ctx past",
                  "ctxT", "o", "rq", "rctxT", "gate", "fin", "ffn gate", "ffn up", "ffn y"):
            filled[n] = sem("filled_" + n.replace(" ", "_"))
            emptied[n] = sem("emptied_" + n.replace(" ", "_"))
        tanh_done = {n: sem("tanh_" + n.replace(" ", "_")) for n in ("ffn gate", "ffn y")}
        split_steps = {n: sem(f"split_steps_{n}") for n in ("q", "k", "rq")}
        parts_stored = {n: sem(f"parts_stored_{n}") for n in ("q", "k", "rq")}
        stacked = {n: sem(f"stacked_{n}") for n in ("q", "k", "rq")}
        max_scored = sem("max_scored")
        max_taken = sem("max_taken")
        scored = sem("scored")
        exp_done = sem("exp_done")
        beats_done = sem("beats_done")
        top_steps = {n: sem(f"top_steps_{n}") for n in MW}
        top_stored = {n: sem(f"top_stored_{n}") for n in MW}
        top_loaded = {n: sem(f"top_loaded_{n}") for n in MW}
        U_filled = {n: sem(f"U_filled_{n}") for n in MW}
        recip_done = {n: sem(f"recip_done_{n}") for n in MW}
        rsum_done = sem("rsum_done")
        mix_done = sem("mix_done")
        gated_steps = sem("gated_steps")
        g_stored = sem("g_stored")
        late_loaded = sem("late_loaded")
        out_stored = sem("out_stored")

        def order(task):
            name, _, n = task.rpartition(" ")
            return (name, int(n)) if n.isdigit() else (task, 0)

        def nth(task, i):
            name, n = order(task)
            return TIMES.get(name, 1) * i + (n + 1)

        def hold(engine, turn):
            if turn is not None:
                engine.nop(nofuse=True)

        def sum_contexts(e, ops, i, t):
            e.wait_ge(emptied["ctx past"], (4 * i + 4).at(t))
            ops.tensor_tensor(ctx_sum[:], ctx_past[:, 0], ctx_past[:, 1], ALU.add).then_inc(rsum_done, 1)

        def mix(e, ops, i, t):
            e.wait_ge(emptied["rctxT"], (i + 1).at(t))
            ops.tensor_tensor(diff[:], rT[:], oT[o_buffer(i)][:], ALU.subtract).then_inc(mix_done, 1)
            ops.tensor_tensor(both[:], rT[:], oT[o_buffer(i)][:], ALU.add).then_inc(mix_done, 1)

        def gate_product(e, ops, i, t):
            e.wait_ge(mix_done, (2 * i + 2).at(t))
            e.wait_ge(emptied["gate"], (i + 1).at(t))
            ops.tensor_tensor(mixed[:], tanh_g[:], diff[:], ALU.mult).then_inc(gated_steps, 1)
            e.wait_ge(gated_steps, (3 * i + 1).at(t))
            ops.tensor_tensor(mixed[:], mixed[:], both[:], ALU.add).then_inc(gated_steps, 1)
            e.wait_ge(late_loaded, (32 * i + 32).at(t))
            e.wait_ge(gated_steps, (3 * i + 2).at(t))
            ops.tensor_tensor(product[:], mixed[:], g_late[:], ALU.mult).then_inc(gated_steps, 1)

        UROUNDS = {"own": 2, "past": 4}
        STACKED = {"q": 128, "k": 96, "rq": 128}

        block = ctx.enter_context(nc.Block())

        @block.sync
        def _(sp):
            def load_x(i, t):
                if i > 0:
                    sp.wait_ge(xn_made, i.at(t))
                src = x[bass.ds(i.at(t), 1)] if t is not None else x[i.c:i.c + 1]
                sp.dma_start(x_in[:], src.rearrange("o (s p) f -> p (o s) f", p=128)).then_inc(x_loaded, 16)

            def stack_parts(dst, src, backwards, raised):
                for par in range(2):
                    v = src.rearrange("j (par d pos) s -> par j d (pos s)", par=2, pos=PAIRS)[par]
                    row = 64 * par
                    for n in (3, 2, 1):
                        take = v[PARTS - n:PARTS] if backwards else v[0:n]
                        sp.dma_start(dst[row:row + n * D].rearrange("p a b -> p (a b)"), take).then_inc(raised, 16)
                        row += n * D

            def store_parts(name, i, t):
                sp.wait_ge(split_steps[name], (4 * i + 4).at(t))
                if i > 0:
                    sp.wait_ge(stacked[name], (STACKED[name] * i).at(t))
                elif name == "rq":
                    sp.wait_ge(past_stacked, 96)
                sp.dma_start(parts_d[name].rearrange("j p s -> p j s"), parts[name][:]).then_inc(parts_stored[name], 16)

            def stack_task(name, i, t, dst, kind):
                if name == "rq" or i > 0:
                    store_parts(name, i, t)
                sp.wait_ge(parts_stored[name], (16 * i + 16).at(t))
                if name == "rq" and rq_buffer(i) == 2:
                    sp.wait_ge(scored, (TILES * (stage("own", i - 1) + 1)).at(t))
                elif i - 1 > 0:
                    sp.wait_ge(scored, (TILES * (stage(kind, i - 2) + 1)).at(t))
                stack_parts(dst, parts_d[name], name == "k", stacked[name])
                if name != "k":
                    n = PARTS * MW[kind]
                    for row in (MAXROW, 64 + MAXROW):
                        sp.dma_start(dst[row:row + n], ones_rows[PARTS:PARTS + n, 0:1, :].to_broadcast([n, PAIRS, S])
                                     ).then_inc(stacked[name], 16)

            def stack_constants(first):
                zeros = slice(PARTS, PARTS + STACK - MAXROW)
                ones = slice(0, STACK - MAXROW)
                fills = [[(stack_k[0], 0, 2, ones), (stack_q[0], 0, 0, zeros)],
                         [(stack_k[1], 0, 2, ones), (stack_q[1], 0, 0, zeros),
                          (stack_rk, 0, 0, slice(0, PARTS)), (stack_rk, PARTS, 1, slice(0, STACK - MAXROW - PARTS)),
                          (stack_rq[0], 0, 0, zeros), (stack_rq[1], 0, 0, zeros)]][first]
                for par in range(2):
                    for stack, row, n, part in fills:
                        row += 64 * par + MAXROW
                        rows = part.stop - part.start
                        sp.dma_start(stack[row:row + rows],
                                     ones_rows[part, n:n + 1, :].to_broadcast([rows, PAIRS, S])).then_inc(ones_loaded, 16)

            def top_task(kind, half, i, t):
                sp.wait_ge(emptied[f"max {kind}"], (2 * i + (half + 1)).at(t))
                if i > 0:
                    sp.wait_ge(top_loaded[kind], (64 * i).at(t))
                tb, r = TB[kind], TR[kind]
                for m in range(tb):
                    sp.dma_start(top_d[kind][half].rearrange("r (c m q) -> m r c q", m=tb, q=128)[m],
                                 topT[kind][m * r:(m + 1) * r, half, :].rearrange("r (c q) -> r c q", q=128)
                                 ).then_inc(top_stored[kind], 16)
                sp.wait_ge(top_stored[kind], (32 * tb * i + 16 * tb * (half + 1)).at(t))
                dst = stack_q[i.c % 2] if kind == "own" else stack_rq[rq_buffer(i)]
                n = MW[kind] * PARTS
                for par in range(2):
                    row = 64 * par + MAXROW
                    sp.dma_start(dst[row:row + n, half * 4:half * 4 + 4, :].rearrange("p a b -> p (a b)"),
                                 top_d[kind][half].rearrange("(par j pos) s -> par j (pos s)", par=2, j=n)[par]
                                 ).then_inc(top_loaded[kind], 16)

            def task(name, i, t):
                p = i.c % 2
                if name == "load x":
                    load_x(i, t)
                elif name in ("store q", "store k"):
                    store_parts(name[-1], i, t)
                elif name == "stack q":
                    stack_task("q", i, t, stack_q[p], "own")
                elif name == "stack k":
                    stack_task("k", i, t, stack_k[p], "own")
                elif name == "stack rq":
                    stack_task("rq", i, t, stack_rq[rq_buffer(i)], "past")
                elif name == "stack constants":
                    stack_constants(1)
                elif name == "stack past":
                    sp.wait_ge(past_split, 4)
                    sp.dma_start(parts_d["rq"].rearrange("j p s -> p j s"), parts["rq"][:]).then_inc(past_stored, 16)
                    sp.wait_ge(past_stored, 16)
                    stack_parts(stack_rk, parts_d["rq"], True, past_stacked)
                elif name.startswith("max"):
                    _, kind, half = name.split()
                    top_task(kind, int(half), i, t)
                elif name == "store g":
                    sp.wait_ge(emptied["ffn y"], (i + 1).at(t))
                    dst = g_d[bass.ds(i.at(t), 1)] if t is not None else g_d[i.c:i.c + 1]
                    sp.dma_start(dst.rearrange("o p s -> p (o s)"), g_new[:]).then_inc(g_stored, 16)
                elif name == "load late":
                    if i.a == 0 and i.c == 0:
                        sp.wait_ge(filled["past T"], 1)
                    sp.wait_ge(g_stored, (16 * i + 16).at(t))
                    if i > 0:
                        sp.wait_ge(out_stored, (16 * i).at(t))
                    src = g_d[bass.ds(i.at(t), 1)] if t is not None else g_d[i.c:i.c + 1]
                    sp.dma_start(g_late[:], src.rearrange("o p s -> p (o s)")).then_inc(late_loaded, 16)
                    src = x[bass.ds(i.at(t), 1)] if t is not None else x[i.c:i.c + 1]
                    sp.dma_start(x_late[:], src.rearrange("o (s p) f -> p (o s) f", p=128)).then_inc(late_loaded, 16)
                elif name == "store out":
                    sp.wait_ge(emptied["fin"], (i + 1).at(t))
                    dst = out[bass.ds(i.at(t), 1)] if t is not None else out[i.c:i.c + 1]
                    sp.dma_start(dst.rearrange("o (s p) f -> p (o s) f", p=128), result[:]).then_inc(out_stored, 16)

            sp.dma_start(x_in[:], x[0].rearrange("(s p) f -> p s f", p=128)).then_inc(x_loaded, 16)
            sp.dma_start(W[:, 0:2, :], weights[:, 0:2, :]).then_inc(qk_weights_loaded, 16)
            sp.dma_start(cols[:], columns).then_inc(qk_weights_loaded, 16)
            sp.dma_start(W[:, 2:, :], weights[:, 2:, :]).then_inc(rest_loaded, 16)
            sp.dma_start(brows[:], rows).then_inc(rest_loaded, 16)
            sp.dma_start(wint[:, 0, :], w_gate).then_inc(rest_loaded, 16)
            sp.dma_start(wint[:, 1, :], w_up).then_inc(rest_loaded, 16)
            sp.dma_start(wint[:, 2, :], w_down).then_inc(rest_loaded, 16)
            sp.dma_start(x_late[:], past.rearrange("(s p) f -> p s f", p=128)).then_inc(rest_loaded, 16)
            sp.wait_ge(ones_rows_made, 4)
            stack_constants(0)

            for slot in first_slots():
                for name, i in slot.sync:
                    task(name, i, None)
            with sp.Fori(0, TURNS) as turn:
                for slot in loop_slots():
                    for name, i in slot.sync:
                        task(name, i, turn)
            for slot in last_slots():
                for name, i in slot.sync:
                    task(name, i, None)
            sp.wait_ge(out_stored, 16 * BATCH)
            sp.wait_ge(g_stored, 16 * BATCH)

        @block.tensor
        def _(pe):
            def free_Z(before, t):
                if before:
                    name, i = before
                    pe.wait_ge(emptied[order(name)[0]], nth(name, i).at(t))

            def transposes(dst, src):
                for st in range(ST):
                    last = nc.tensor.transpose(dst[:, st * 128:(st + 1) * 128], src[:, st, :], ident[:])
                return last

            def small_task(name, i, before, t):
                kind, n = order(name)
                done = filled[kind]
                first = i.a == 0 and i.c == 0
                if kind == "past k" or kind == "past v":
                    pe.wait_ge(emptied["past T"], 1)
                elif kind == "q" and first:
                    pe.wait_ge(qk_weights_loaded, 32)
                elif kind == "v" and first:
                    pe.wait_ge(rest_loaded, 96)
                elif kind == "ffn gate" and first:
                    pe.wait_ge(weights_ready, 4)
                elif kind == "xnT" and first:
                    pe.wait_ge(ident_steps, 2)
                if kind == "xnT":
                    pe.wait_ge(xn_made, (i + 1).at(t))
                elif kind in ("q", "k", "v"):
                    pe.wait_ge(emptied["xnT"], (i + 1).at(t))
                elif kind in ("max own", "max past"):
                    pe.wait_ge(top_steps[kind[4:]], (8 * i + 4 * (n + 1)).at(t))
                elif kind in ("ctx own", "ctx past"):
                    pe.wait_ge(U_filled[kind[4:]], nth(name, i).at(t))
                elif kind == "ctxT":
                    pe.wait_ge(emptied["ctx own"], (2 * i + 2).at(t))
                elif kind == "o":
                    pe.wait_ge(emptied["ctxT"], (i + 1).at(t))
                elif kind == "rq":
                    pe.wait_ge(emptied["o"], (i + 1).at(t))
                elif kind == "rctxT":
                    pe.wait_ge(rsum_done, (i + 1).at(t))
                elif kind == "gate":
                    pe.wait_ge(emptied["rctxT"], (i + 1).at(t))
                elif kind == "fin":
                    pe.wait_ge(gated_steps, (3 * i + 3).at(t))
                elif kind == "ffn gate":
                    pe.wait_ge(emptied["xnT"], (i + 1).at(t))
                elif kind == "ffn up":
                    pe.wait_ge(emptied["ffn gate"], nth("ffn gate %d" % n, i).at(t))
                elif kind == "ffn y":
                    pe.wait_ge(emptied["ffn up"], (NB * i + NB).at(t))
                free_Z(before, t)
                if kind == "past T":
                    last = transposes(Z, x_late)
                elif kind == "past k":
                    last = nc.tensor.matmul(Z[:], Wrk, rT[:], start=True, stop=True)
                elif kind == "past v":
                    for st in range(ST):
                        last = nc.tensor.matmul(Z[:, st * H:(st + 1) * H], rT[:, st * 128:(st + 1) * 128], Wrv,
                                                start=True, stop=True)
                elif kind == "xnT":
                    last = transposes(Z, xn)
                elif kind == "q":
                    last = nc.tensor.matmul(Z[:], Wq, xnT[:], start=True, stop=True)
                elif kind == "k":
                    last = nc.tensor.matmul(Z[:], Wk, xnT[:], start=True, stop=True)
                elif kind == "v":
                    for st in range(ST):
                        last = nc.tensor.matmul(Z[:, st * H:(st + 1) * H], xnT[:, st * 128:(st + 1) * 128], Wv,
                                                start=True, stop=True)
                elif kind in ("max own", "max past"):
                    tb = TB[kind[4:]]
                    for c in range(ST // tb):
                        last = nc.tensor.transpose(
                            Zb[0:96, c * 128:(c + 1) * 128],
                            top_parts[kind[4:]][:, n, c * tb:(c + 1) * tb].rearrange("p s m j c -> p (s m j c)"), identb[:])
                elif kind in ("ctx own", "ctx past"):
                    src = U[:, n % 2, :].rearrange("p (s q) -> p s q", s=ST)
                    last = transposes(Z, src)
                elif kind == "ctxT":
                    last = transposes(Z, ctx_own)
                elif kind == "o":
                    last = nc.tensor.matmul(Z[:], Wo, ctxT[:], start=True, stop=True)
                elif kind == "rq":
                    last = nc.tensor.matmul(Z[:], Wrq, oT[o_buffer(i)][:], start=True, stop=True)
                elif kind == "rctxT":
                    last = transposes(Z, ctx_sum)
                elif kind == "gate":
                    nc.tensor.matmul(Z[:], Wg_own, oT[o_buffer(i)][:], start=True, stop=False)
                    last = nc.tensor.matmul(Z[:], Wg_past, rT[:], start=False, stop=True)
                elif kind == "fin":
                    last = transposes(Z, product[:].rearrange("p (s q) -> p s q", s=ST))
                elif kind == "ffn gate":
                    last = nc.tensor.matmul(Z[:], wffn[:, 0, n * 128:(n + 1) * 128], xnT[:], start=True, stop=True)
                elif kind == "ffn up":
                    last = nc.tensor.matmul(Z[:], wffn[:, 1, n * 128:(n + 1) * 128], xnT[:], start=True, stop=True)
                elif kind == "ffn y":
                    for b in range(NB):
                        last = nc.tensor.matmul(Z[:], wffn[:, 2, b * 128:(b + 1) * 128], hT[:, b, :],
                                                start=(b == 0), stop=(b == NB - 1))
                last.then_inc(done, 1)

            def maxima_tile(kind, i, s, beat, j, t):
                group, st = divmod(beat, ST)
                u = MAXIMA_ORDER[j]
                pos, row = 2 * group + u // 2, 64 * (u % 2)
                n = QUAD * beat + j
                qs, ks = (stack_q[i.c % 2], stack_k[i.c % 2]) if kind == "own" else (stack_rq[rq_buffer(i)], stack_rk)
                if n == 0:
                    if kind == "own" and i.a == 0 and i.c < 2:
                        pe.wait_ge(ones_loaded, 64 if i.c == 0 else 256)
                    if kind == "own":
                        pe.wait_ge(stacked["q"], (STACKED["q"] * (i + 1)).at(t))
                        pe.wait_ge(stacked["k"], (STACKED["k"] * (i + 1)).at(t))
                    else:
                        pe.wait_ge(stacked["rq"], (STACKED["rq"] * (i + 1)).at(t))
                        if i.a == 0 and i.c == 0:
                            pe.wait_ge(past_stacked, 96)
                if in_ring(s, n) > 0:
                    pe.wait_ge(max_taken, in_ring(s, n).at(t))
                nc.tensor.matmul(MX[BANK[n]][:], qs[row:row + STACK, pos, st * 128:(st + 1) * 128],
                                 ks[row:row + STACK, pos, :], start=True, stop=True).then_inc(max_scored, 1)

            def score_tile(kind, i, s, beat, j, t):
                group, st = divmod(beat, ST)
                u = SCORES_ORDER[j]
                pos, row = 2 * group + u // 2, 64 * (u % 2)
                n = QUAD * beat + j
                qs, ks = (stack_q[i.c % 2], stack_k[i.c % 2]) if kind == "own" else (stack_rq[rq_buffer(i)], stack_rk)
                if n == 0:
                    pe.wait_ge(top_loaded[kind], (64 * i + 32).at(t))
                if n == TILES // 2:
                    pe.wait_ge(top_loaded[kind], (64 * i + 64).at(t))
                if in_ring(s, n) > 0:
                    pe.wait_ge(exp_done, in_ring(s, n).at(t))
                nc.tensor.matmul(SC[BANK[n]][:], ks[row:row + STACK, pos, st * 128:(st + 1) * 128],
                                 qs[row:row + STACK, pos, :], start=True, stop=True).then_inc(scored, 1)

            def weigh_values(kind, i, s, beat, U_before, t):
                group, st = divmod(beat, ST)
                vals = values[i.c % 2] if kind == "own" else past_values
                per = ST * GROUPS // UROUNDS[kind]
                pe.wait_ge(exp_done, (TILES * s + 4 * (beat + 1)).at(t))
                if beat == 0 and kind == "own":
                    pe.wait_ge(emptied["v"], (i + 1).at(t))
                if beat == 0 and kind == "past" and i.a == 0 and i.c == 0:
                    pe.wait_ge(emptied["past v"], 1)
                if beat % per == 0 and U_before:
                    k0, v0 = U_before
                    pe.wait_ge(U_filled[k0], v0.at(t))
                for u in range(QUAD):
                    last = nc.tensor.matmul(CT[32 * u:32 * u + 32, :], vals[:, st, FIRST_HEAD[group] + u, :],
                                            probs[:, beat % PBUF, u, :], start=(beat % per == 0),
                                            stop=(beat % per == per - 1), skip_group_check=True)
                last.then_inc(beats_done, 1)

            def run(slots, before, pending, U_before, t):
                for slot in slots:
                    E = slot.probs
                    for b in range(BEATS):
                        M = slot.maxima_of(b)
                        for j in range(QUAD):
                            if M:
                                maxima_tile(*M[0], stage(*M[0]), M[1], j, t)
                            if E:
                                score_tile(*E, stage(*E), b, j, t)
                            if j == 1 and pending:
                                kind, i, beat = pending
                                weigh_values(kind, i, stage(kind, i), beat, U_before, t)
                                per = BEATS // UROUNDS[kind]
                                if beat % per == per - 1:
                                    U_before = (kind, UROUNDS[kind] * i + (beat // per + 1))
                        if b in slot.small:
                            name, i = slot.small[b]
                            small_task(name, i, before, t)
                            before = (name, i)
                        pending = (*E, b) if E else None
                return before, pending, U_before

            before, pending, U_before = run(first_slots(), None, None, None, None)
            i = Count(2, LOOP_FIRST)
            with pe.Fori(0, TURNS) as turn:
                run(loop_slots(), (before[0], i), ("past", i - 2, BEATS - 1), ("past", 4 * (i - 2) + 3), turn)
            i = Count(0, LOOP_FIRST + 2 * TURNS)
            run(last_slots(), (before[0], i), ("past", i - 2, BEATS - 1), ("past", 4 * (i - 2) + 3), None)

        @block.scalar
        def _(act):
            def probabilities(kind, i, s, beat, j, t):
                n, u = QUAD * beat + j, SCORES_ORDER[j]
                act.wait_ge(scored, (TILES * s + (n + 1)).at(t))
                if j == 0 and BEATS * s + (beat - PBUF + 1) > 0:
                    act.wait_ge(beats_done, (BEATS * s + (beat - PBUF + 1)).at(t))
                nc.scalar.activation(probs[:, beat % PBUF, u, :], SC[BANK[n]][:], ACT.Exp,
                                     scale=SCALE).then_inc(exp_done, 1)

            def take_contexts(kind, i, s, beat, t):
                n = beat // (BEATS // UROUNDS[kind])
                act.wait_ge(beats_done, (BEATS * s + (beat + 1)).at(t))
                nc.scalar.activation(U[:, n % 2, :], CT[:], ACT.Copy).then_inc(U_filled[kind], 1)

            def small_task(name, i, t):
                kind, n = order(name)
                p = i.c % 2
                if kind in ("v", "past v", "ctx own", "ctx past", "fin", "ffn up"):
                    return
                act.wait_ge(filled[kind], nth(name, i).at(t))
                if kind == "past T":
                    nc.scalar.activation(rT[:], Z[:], ACT.Copy).then_inc(emptied[kind], 1)
                elif kind == "past k":
                    nc.scalar.activation(flat["rq"][:], Z[:], ACT.Identity, bias=brk).then_inc(emptied[kind], 1)
                elif kind == "xnT":
                    nc.scalar.activation(xnT[:], Z[:], ACT.Copy).then_inc(emptied[kind], 1)
                elif kind in ("q", "k", "rq"):
                    if i > 0:
                        act.wait_ge(split_steps[kind], (4 * i).at(t))
                    elif kind == "rq":
                        act.wait_ge(past_split, 4)
                    nc.scalar.activation(flat[kind][:], Z[:], ACT.Identity,
                                         bias={"q": bq, "k": bk, "rq": brq}[kind]).then_inc(emptied[kind], 1)
                elif kind in ("max own", "max past"):
                    nc.scalar.activation(topT[kind[4:]][:, n, :], Zb[0:96, 0:S // TB[kind[4:]]],
                                         ACT.Copy).then_inc(emptied[kind], 1)
                elif kind == "ctxT":
                    nc.scalar.activation(ctxT[:], Z[:], ACT.Copy).then_inc(emptied[kind], 1)
                elif kind == "o":
                    nc.scalar.activation(oT[o_buffer(i)][:], Z[:], ACT.Identity, bias=bo).then_inc(emptied[kind], 1)
                elif kind == "rctxT":
                    nc.scalar.activation(rT[:], Z[:], ACT.Copy, scale=1.0 / PAST).then_inc(emptied[kind], 1)
                elif kind == "gate":
                    nc.scalar.activation(tanh_g[:], Z[:], ACT.Tanh, bias=half_bg[:], scale=0.5).then_inc(emptied[kind], 1)
                elif kind in ("ffn gate", "ffn y"):
                    nc.scalar.activation(tanh_f[:], Z[:], ACT.Tanh, scale=0.5).then_inc(tanh_done[kind], 1)

            def run(slots, pending, t):
                for slot in slots:
                    E = slot.probs
                    for b in range(BEATS):
                        if E:
                            for j in (0, 1):
                                probabilities(*E, stage(*E), b, j, t)
                        if pending:
                            kind, i, beat = pending
                            per = BEATS // UROUNDS[kind]
                            if beat % per == per - 1:
                                take_contexts(kind, i, stage(kind, i), beat, t)
                        if E:
                            for j in (2, 3):
                                probabilities(*E, stage(*E), b, j, t)
                        if b in slot.small:
                            small_task(*slot.small[b], t)
                        pending = (*E, b) if E else None

            act.wait_ge(qk_weights_loaded, 32)
            nc.scalar.activation(half_bg[:], bg, ACT.Copy, scale=0.5).then_inc(half_bg_made, 1)
            act.wait_ge(half_bg_made, 1)

            run(first_slots(), None, None)
            i = Count(2, LOOP_FIRST)
            with act.Fori(0, TURNS) as turn:
                run(loop_slots(), ("past", i - 2, BEATS - 1), turn)
            run(last_slots(), ("past", Count(0, LOOP_FIRST + 2 * TURNS - 2), BEATS - 1), None)

        @block.vector
        def _(dve):
            def take_maxima(kind, i, s, beat, j, t):
                group, st = divmod(beat, ST)
                u = MAXIMA_ORDER[j]
                pos, par, n = 2 * group + u // 2, u % 2, QUAD * beat + j
                half, c = divmod(pos, PAIRS // 2)
                if n % (TILES // 2) == 0 and i > 0:
                    dve.wait_ge(top_steps[kind], (8 * i - (4 if n == 0 else 0)).at(t))
                dve.wait_ge(max_scored, (TILES * s + (n + 1)).at(t))
                nc.vector.tensor_reduce(top[kind][:, half, st, par, :, c],
                                        MX[BANK[n]][:].rearrange("p (w k) -> p w k", w=MW[kind]),
                                        AX_X, ALU.max, negate=True).then_inc(max_taken, 1)

            def small_task(name, i, t):
                kind, n = order(name)
                last_sequence = i.a == 0 and i.c == BATCH - 1
                if kind == "past v":
                    dve.wait_ge(filled[kind], 1)
                    dve.wait_ge(values_ready, 6)
                    for a in range(2):
                        last = nc.vector.tensor_tensor(
                            past_values[:, 2 * a:2 * a + 2, :, SLOT * a:SLOT * a + D],
                            Zt[:, 2 * a:2 * a + 2, :].rearrange("p s (h d) -> p s h d", d=D),
                            brows[:, 1:2, :].rearrange("p o (h d) -> p o h d", d=D).to_broadcast([128, 2, HEADS, D]),
                            ALU.add)
                    last.then_inc(emptied[kind], 1)
                elif kind == "v":
                    dve.wait_ge(filled[kind], (i + 1).at(t))
                    if i.a == 0 and i.c == 0:
                        dve.wait_ge(values_ready, 6)
                    if i - 1 > 0:
                        dve.wait_ge(beats_done, (BEATS * (stage("own", i - 2) + 1)).at(t))
                    for a in range(2):
                        last = nc.vector.tensor_tensor(
                            values[i.c % 2][:, :, 8 * a:8 * a + 8, SLOT * a:SLOT * a + D],
                            Zt[:, :, 64 * a:64 * a + 64].rearrange("p s (h d) -> p s h d", d=D),
                            brows[:, 0:1, 64 * a:64 * a + 64].rearrange("p o (h d) -> p o h d", d=D).to_broadcast([128, ST, 8, D]),
                            ALU.add)
                    last.then_inc(emptied[kind], 1)
                elif kind in ("ctx own", "ctx past"):
                    k2 = kind[4:]
                    dve.wait_ge(filled[kind], nth(name, i).at(t))
                    if k2 == "past" and n == 0 and i > 0:
                        dve.wait_ge(rsum_done, i.at(t))
                    zc = Z[:].rearrange("p (s q c) -> p s q c", s=ST, q=QUAD)
                    nc.vector.reciprocal(recip[:], zc[:, :, :, D:D + SLOT + 1:SLOT]).then_inc(recip_done[k2], 1)
                    dve.wait_ge(recip_done[k2], nth(name, i).at(t))
                    for a in range(2):
                        if k2 == "own":
                            c0 = (FIRST_HEAD[2 * n + a]) * D
                            dst = ctx_own[:, :, c0:c0 + QUAD * D]
                        else:
                            c0 = FIRST_HEAD[n] * D
                            dst = ctx_past[:, a, :, c0:c0 + QUAD * D]
                        last = nc.vector.tensor_tensor(dst.rearrange("p s (q d) -> p s q d", d=D),
                                                       zc[:, :, :, SLOT * a:SLOT * a + D],
                                                       recip[:, :, :, a:a + 1].to_broadcast([128, ST, QUAD, D]), ALU.mult)
                    last.then_inc(emptied[kind], 1)
                    if name == "ctx past 3" and last_sequence:
                        sum_contexts(dve, nc.vector, i, t)
                elif kind == "rctxT" and last_sequence:
                    mix(dve, nc.vector, i, t)
                elif kind == "gate" and last_sequence:
                    gate_product(dve, nc.vector, i, t)
                elif kind == "fin":
                    dve.wait_ge(filled[kind], (i + 1).at(t))
                    dve.wait_ge(late_loaded, (32 * i + 32).at(t))
                    nc.vector.scalar_tensor_tensor(out=result[:], in0=Zt, scalar=0.25, in1=x_late[:],
                                                   op0=ALU.mult, op1=ALU.add).then_inc(emptied[kind], 1)
                elif kind == "ffn gate":
                    dve.wait_ge(tanh_done[kind], nth(name, i).at(t))
                    nc.vector.scalar_tensor_tensor(out=hg[:], in0=tanh_f[:], scalar=1.0, in1=Z[:],
                                                   op0=ALU.add, op1=ALU.mult).then_inc(emptied[kind], 1)
                elif kind == "ffn up":
                    dve.wait_ge(filled[kind], nth(name, i).at(t))
                    nc.vector.tensor_tensor(hT[:, n, :], hg[:], Z[:], ALU.mult).then_inc(emptied[kind], 1)
                elif kind == "ffn y":
                    dve.wait_ge(tanh_done[kind], (i + 1).at(t))
                    if i > 0:
                        dve.wait_ge(g_stored, (16 * i).at(t))
                    nc.vector.scalar_tensor_tensor(out=g_new[:], in0=tanh_f[:], scalar=1.0, in1=Z[:],
                                                   op0=ALU.add, op1=ALU.mult).then_inc(emptied[kind], 1)

            def statistics(i, t):
                dve.wait_ge(x_loaded, (16 * i + 16).at(t))
                for st in range(ST):
                    last = nc.vector.bn_stats(bn[:, st, :], x_in[:, st, :])
                last.then_inc(bn_done, 1)
                dve.wait_ge(bn_done, (i + 1).at(t))
                if i > 0:
                    dve.wait_ge(xn_made, i.at(t))
                hold(dve, t)
                for st in range(ST):
                    last = nc.vector.bn_aggr(mean_var[:, st, :], bn[:, st, :])
                last.then_inc(stats_done, 1)

            def run(slots, late, t):
                for slot in slots:
                    for b in range(BEATS):
                        M = slot.maxima_of(b)
                        if M:
                            for j in (0, 1):
                                take_maxima(*M[0], stage(*M[0]), M[1], j, t)
                        if slot.stats and slot.stats[0] == b:
                            statistics(slot.stats[1], t)
                        if late:
                            small_task(*late, t)
                        if M:
                            for j in (2, 3):
                                take_maxima(*M[0], stage(*M[0]), M[1], j, t)
                        late = slot.small.get(b)
                return late

            half_keys = S // PAST
            nc.vector.memset(ones_rows[:], 0.0).then_inc(ones_rows_made, 1)
            dve.wait_ge(ones_rows_made, 1)
            nc.vector.memset(ones_rows[0:PARTS, 0, 0:half_keys], 1.0).then_inc(ones_rows_made, 1)
            nc.vector.memset(ones_rows[0:PARTS, 1, half_keys:S], 1.0).then_inc(ones_rows_made, 1)
            nc.vector.memset(ones_rows[0:PARTS, 2, :], 1.0).then_inc(ones_rows_made, 1)
            statistics(Count(0, 0), None)
            dve.wait_ge(rstd_steps, 2)
            for st in range(ST):
                last = nc.vector.tensor_scalar(xn[:, st, :], x_in[:, st, :], mean_var[:, st, 0:1],
                                               rstd[:, st:st + 1], ALU.subtract, ALU.mult)
            last.then_inc(xn_made, 1)
            dve.wait_ge(rest_loaded, 96)
            for n in range(2):
                nc.vector.tensor_scalar(wffn[:, n, :], wint[:, n, :], DEQUANT, None, ALU.mult).then_inc(weights_ready, 1)
            nc.vector.tensor_scalar(wffn[:, 2, :], wint[:, 2, :], DEQUANT, 0.5, ALU.mult, ALU.mult).then_inc(weights_ready, 1)
            dve.wait_ge(ident_steps, 2)
            nc.vector.tensor_copy(identb[:], ident[:]).then_inc(weights_ready, 1)
            for n in ("q", "k"):
                part = [parts[n][:, j, :] for j in (range(PARTS) if n == "q" else reversed(range(PARTS)))]
                dve.wait_ge(emptied[n], 1)
                if n == "k":
                    dve.wait_ge(split_steps["q"], 4)
                nc.vector.tensor_copy(part[0], flat[n][:]).then_inc(split_steps[n], 1)
                dve.wait_ge(split_steps[n], 1)
                nc.vector.tensor_tensor(rest[:], flat[n][:], part[0], ALU.subtract).then_inc(split_steps[n], 1)
                dve.wait_ge(split_steps[n], 2)
                nc.vector.tensor_copy(part[1], rest[:]).then_inc(split_steps[n], 1)
                dve.wait_ge(split_steps[n], 3)
                nc.vector.tensor_tensor(part[2], rest[:], part[1], ALU.subtract).then_inc(split_steps[n], 1)

            late = run(first_slots(), None, None)
            i = Count(2, LOOP_FIRST)
            with dve.Fori(0, TURNS) as turn:
                run(loop_slots(), (late[0], i), turn)
            run(last_slots(), (late[0], Count(0, LOOP_FIRST + 2 * TURNS)), None)

        @block.gpsimd
        def _(pool):
            def split(src, res, out_parts, raised, base, t):
                hold(pool, t)
                nc.gpsimd.tensor_copy(out_parts[0], src).then_inc(raised, 1)
                pool.wait_ge(raised, (base + 1).at(t))
                nc.gpsimd.tensor_tensor(res, src, out_parts[0], ALU.subtract).then_inc(raised, 1)
                pool.wait_ge(raised, (base + 2).at(t))
                hold(pool, t)
                nc.gpsimd.tensor_copy(out_parts[1], res).then_inc(raised, 1)
                pool.wait_ge(raised, (base + 3).at(t))
                nc.gpsimd.tensor_tensor(out_parts[2], res, out_parts[1], ALU.subtract).then_inc(raised, 1)

            def top_split(kind, half, i, t):
                s = stage(kind, i)
                src = top[kind][:, half].rearrange("p s r w c -> p (s r w) c")
                dst = top_parts[kind][:, half].rearrange("p s m j c -> p (s m) j c")
                if i > 0:
                    pool.wait_ge(filled[f"max {kind}"], (2 * i + (half - 1)).at(t))
                pool.wait_ge(max_taken, (TILES * s + TILES // 2 * (half + 1)).at(t))
                split(src, top_rest[kind][:], [dst[:, :, j, :] for j in range(PARTS)],
                      top_steps[kind], 8 * i + 4 * half, t)

            def value_operands():
                for v in (values[0], values[1], past_values):
                    nc.gpsimd.memset(v[:], 0.0).then_inc(values_cleared, 1)
                pool.wait_ge(values_cleared, 3)
                for a in range(2):
                    for v in (values[0], values[1]):
                        nc.gpsimd.memset(v[:, :, 8 * a:8 * a + 8, SLOT * a + D:SLOT * a + D + 1], 1.0).then_inc(values_ready, 1)
                    nc.gpsimd.memset(past_values[:, 2 * a:2 * a + 2, :, SLOT * a + D:SLOT * a + D + 1], 1.0).then_inc(values_ready, 1)

            def task(name, i, t):
                if name.startswith("max"):
                    _, kind, half = name.split()
                    top_split(kind, int(half), i, t)
                elif name == "split past":
                    pool.wait_ge(emptied["past k"], 1)
                    pool.wait_ge(split_steps["k"], 4)
                    split(flat["rq"][:], rest[:], [parts["rq"][:, j, :] for j in reversed(range(PARTS))],
                          past_split, Count(0, 0), None)
                elif name.startswith("split"):
                    n = name.split()[1]
                    if i > 0:
                        pool.wait_ge(parts_stored[n], (16 * i).at(t))
                    elif n == "rq":
                        pool.wait_ge(past_stored, 16)
                    pool.wait_ge(emptied[n], (i + 1).at(t))
                    split(flat[n][:], rest[:], [parts[n][:, j, :] for j in
                                                (range(PARTS) if n != "k" else reversed(range(PARTS)))],
                          split_steps[n], 4 * i, t)
                elif name == "xn":
                    pool.wait_ge(stats_done, (i + 1).at(t))
                    hold(pool, t)
                    nc.gpsimd.tensor_scalar(var_eps[:], mean_var[:, :, 1], EPS, None, ALU.add).then_inc(rstd_steps, 1)
                    pool.wait_ge(rstd_steps, (2 * i + 1).at(t))
                    nc.gpsimd.tensor_tensor(rstd[:], var_eps[:], minus_half[:], ALU.pow).then_inc(rstd_steps, 1)
                    if i.a == 0 and i.c == 0:
                        value_operands()
                        return
                    if i > 0:
                        pool.wait_ge(filled["xnT"], i.at(t))
                    pool.wait_ge(rstd_steps, (2 * i + 2).at(t))
                    hold(pool, t)
                    for st in range(ST):
                        last = nc.gpsimd.tensor_scalar(xn[:, st, :], x_in[:, st, :], mean_var[:, st, 0:1],
                                                       rstd[:, st:st + 1], ALU.subtract, ALU.mult)
                    last.then_inc(xn_made, 1)
                elif name == "rsum":
                    sum_contexts(pool, nc.gpsimd, i, t)
                elif name == "mix":
                    mix(pool, nc.gpsimd, i, t)
                elif name == "gated":
                    gate_product(pool, nc.gpsimd, i, t)

            nc.gpsimd.memset(ident[:], 0.0).then_inc(ident_steps, 1)
            nc.gpsimd.memset(minus_half[:], -0.5).then_inc(minus_half_made, 1)
            pool.wait_ge(ident_steps, 1)
            nc.gpsimd.affine_select(out=ident[:], in_=ident[:], compare_op=ALU.not_equal, fill=1.0, base=0,
                                    pattern=[[-1, 128]], channel_multiplier=1).then_inc(ident_steps, 1)
            pool.wait_ge(minus_half_made, 1)

            for slot in first_slots():
                for name, i in slot.pool:
                    task(name, i, None)
            with pool.Fori(0, TURNS) as turn:
                for slot in loop_slots():
                    for name, i in slot.pool:
                        task(name, i, turn)
            for slot in last_slots():
                for name, i in slot.pool:
                    task(name, i, None)
    return nc


def kernel(**inputs):
    import numpy as np
    import concourse.bacc as bacc
    from concourse.bass_utils import run_bass_kernel_spmd

    a = {n.removeprefix("L0_"): np.asarray(v) for n, v in inputs.items()}
    order = []
    for par in range(2):
        for d in range(D):
            for pos in range(PAIRS):
                head = FIRST_HEAD[pos // 2] + 2 * (pos % 2) + par
                order.append(head * D + d)
    order = np.array(order)
    gate = a["attn_Wg"]
    weights = np.stack([a["attn_Wq"][:, order], a["attn_Wk"][:, order], a["attn_Wv"], a["attn_Wo"],
                        a["attn_Wrq"][:, order], a["attn_Wrk"][:, order], a["attn_Wrv"], gate[:H], gate[H:]], axis=1)
    columns = np.stack([a["attn_bq"][order], a["attn_bk"][order], a["attn_bo"], a["attn_brq"][order],
                        a["attn_brk"][order], a["attn_bg"]], axis=1)
    rows = np.broadcast_to(np.stack([a["attn_bv"], a["attn_brv"]])[None], (128, 2, H))
    down = a["ffn_w_down"].T.reshape(NB, 128, H).transpose(1, 0, 2).reshape(128, NB * H)
    arrays = {
        "x": a["attn_hidden_states"], "past": a["attn_past_states"].reshape(S, H), "weights": weights,
        "columns": columns, "rows": rows, "w_gate": a["ffn_w_gate"].T, "w_up": a["ffn_w_up"].T, "w_down": down,
    }
    arrays = {n: np.ascontiguousarray(v) for n, v in arrays.items()}
    nc = bacc.Bacc("TRN2", target_bir_lowering=False, num_devices=1)
    nc.disable_value_cache = True
    args = [nc.dram_tensor(n, v.shape, mybir.dt.from_np(v.dtype), kind="ExternalInput").ap() for n, v in arrays.items()]
    out = nc.dram_tensor("out", (BATCH, S, H), F32, kind="ExternalOutput").ap()
    build(nc, *args, out)
    r = run_bass_kernel_spmd(nc, [arrays], core_ids=[0])
    return r.results[0]["out"]
```
